# Optimizing a Trainium2 kernel written in Bass

```python
import numpy as np
import jax
import jax.numpy as jnp

def _softmax(x, axis=-1):
    return jax.nn.softmax(x, axis=axis)

def _gelu(x):
    return jax.nn.gelu(x, approximate=True)

def _silu(x):
    return jax.nn.silu(x)

def _sigmoid(x):
    return jax.nn.sigmoid(x)

def _layernorm(x, axis=-1, eps=1e-05):
    m = jnp.mean(x, axis=axis, keepdims=True)
    v = jnp.var(x, axis=axis, keepdims=True)
    return (x - m) / jnp.sqrt(v + eps)

def _scatter_add(tgt, idx, src, axis=0):
    return tgt.at[idx].add(src)

def _segment_sum(src, seg, n):
    return jax.ops.segment_sum(src, seg, n)
kernel_name = 'mk_adj_resnorm_d4_adj_r2_caba33'

def setup_inputs(seed: int=0):
    np.random.seed(seed)
    _w = jnp.asarray

    def _rec_inputs():
        import jax
        import jax.numpy as jnp
        _gk = jax.random.key(seed)
        x = 7.22e-05 + 1 * jax.random.normal(jax.random.fold_in(_gk, 1), (32, 256, 256), jnp.float32)
        _a = jax.random.bernoulli(jax.random.fold_in(_gk, 2), 0.0078125, (32, 256, 256))
        _a = jnp.logical_or(_a, jnp.swapaxes(_a, -1, -2))
        _a = jnp.logical_or(_a, jnp.eye(256, dtype=bool))
        _af = _a.astype(jnp.float32)
        _af = _af * jax.random.uniform(jax.random.fold_in(_gk, 3), (32, 256, 256), jnp.float32, 0.05, 1)
        adj = _af
        return (x, adj)
    x, adj = _rec_inputs()

    def _L0_gnn_setup():
        import jax, jax.numpy as jnp
        import numpy as np
        B, N, D = (8, 1024, 256)
        key = jax.random.key(seed)
        ks = jax.random.split(key, 8)
        scale = 0.5 / np.sqrt(D)
        x = jax.random.normal(ks[0], (B, N, D), dtype=jnp.float32)
        adj = jax.random.uniform(ks[1], (B, N, N), dtype=jnp.float32)
        Wq_w = jax.random.normal(ks[2], (D, D), dtype=jnp.float32) * scale
        Wk_w = jax.random.normal(ks[3], (D, D), dtype=jnp.float32) * scale
        Wv_w = jax.random.normal(ks[4], (D, D), dtype=jnp.float32) * scale
        Wq_b = jnp.zeros((D,), dtype=jnp.float32)
        Wk_b = jnp.zeros((D,), dtype=jnp.float32)
        Wv_b = jnp.zeros((D,), dtype=jnp.float32)
        return {'x': x, 'adj': adj, 'Wq_w': Wq_w, 'Wq_b': Wq_b, 'Wk_w': Wk_w, 'Wk_b': Wk_b, 'Wv_w': Wv_w, 'Wv_b': Wv_b}
    _L0_gnn_all = _L0_gnn_setup()
    _L0_gnn_in = {k: v for k, v in _L0_gnn_all.items() if k in ('Wq_w', 'Wq_b', 'Wk_w', 'Wk_b', 'Wv_w', 'Wv_b')}
    del _L0_gnn_all

    def _L1_gnn_setup():
        import jax, jax.numpy as jnp
        import numpy as np
        B, N, DIN, DOUT, K = (4, 1024, 256, 256, 3)
        key = jax.random.key(seed)
        ks = jax.random.split(key, 8)
        X = jax.random.normal(ks[0], (B, N, DIN), dtype=jnp.float32)
        A = jax.random.uniform(ks[1], (B, N, N), dtype=jnp.float32)
        Wv = jax.random.normal(ks[2], (DIN, DOUT), dtype=jnp.float32) * 0.02
        bv = jax.random.normal(ks[3], (DOUT,), dtype=jnp.float32) * 0.02
        aw = jax.random.normal(ks[4], (2 * DOUT, 1), dtype=jnp.float32) * 0.05
        ab = jax.random.normal(ks[5], (1,), dtype=jnp.float32) * 0.05
        Wk = jax.random.normal(ks[6], (K, DIN, DOUT), dtype=jnp.float32) * 0.02
        bk = jax.random.normal(ks[7], (K, DOUT), dtype=jnp.float32) * 0.02
        return {'X': X, 'A': A, 'Wv': Wv, 'bv': bv, 'aw': aw, 'ab': ab, 'Wk': Wk, 'bk': bk}
    _L1_gnn_all = _L1_gnn_setup()
    _L1_gnn_in = {k: v for k, v in _L1_gnn_all.items() if k in ('Wv', 'bv', 'aw', 'ab', 'Wk', 'bk')}
    del _L1_gnn_all

    def _L2_gnn_setup():
        import jax, jax.numpy as jnp
        import numpy as np
        EPS_LN = 1e-05

        def hypergraph_conv(x, adj, W, b):
            N, C, _ = adj.shape
            H = (adj != 0).astype(x.dtype)
            w = adj.reshape(N, -1)[:, :C]
            xw = jnp.einsum('ncd,hd->nch', x, W)
            Dn = jnp.einsum('nce,ne->nc', H, w)
            Dn = jnp.where(Dn > 0, 1.0 / Dn, 0.0)
            Be = H.sum(axis=1)
            Be = jnp.where(Be > 0, 1.0 / Be, 0.0)
            m = Be[:, :, None] * jnp.einsum('nce,nch->neh', H, xw)
            out = Dn[:, :, None] * jnp.einsum('nce,neh->nch', H, m)
            return out + b

        def layer_norm(x, g, b):
            mu = jnp.mean(x, axis=-1, keepdims=True)
            var = jnp.var(x, axis=-1, keepdims=True)
            return (x - mu) * jax.lax.rsqrt(var + EPS_LN) * g + b
        key = jax.random.key(seed)
        ks = jax.random.split(key, 4)
        N, C, Din, Dh, Dout = (16, 512, 256, 512, 256)
        x = jax.random.normal(ks[0], (N, C, Din), dtype=jnp.float32)
        adj = jax.random.uniform(ks[1], (N, C, C), dtype=jnp.float32, minval=0.1, maxval=1.0)
        W1 = jax.random.normal(ks[2], (Dh, Din), dtype=jnp.float32) * (1.0 / np.sqrt(Din))
        b1 = jnp.zeros((Dh,), dtype=jnp.float32)
        gamma = jnp.ones((Dh,), dtype=jnp.float32)
        beta = jnp.zeros((Dh,), dtype=jnp.float32)
        W2 = jax.random.normal(ks[3], (Dout, Dh), dtype=jnp.float32) * (1.0 / np.sqrt(Dh))
        b2 = jnp.zeros((Dout,), dtype=jnp.float32)
        return {'x': x, 'adj': adj, 'W1': W1, 'b1': b1, 'gamma': gamma, 'beta': beta, 'W2': W2, 'b2': b2}
    _L2_gnn_all = _L2_gnn_setup()
    _L2_gnn_in = {k: v for k, v in _L2_gnn_all.items() if k in ('W1', 'b1', 'gamma', 'beta', 'W2', 'b2')}
    del _L2_gnn_all

    def _L3_gnn_setup():
        import jax, jax.numpy as jnp
        import numpy as np
        EPS = 1e-06
        key = jax.random.key(seed)
        k1, k2, k3 = jax.random.split(key, 3)
        B, N, F, O = (8, 2048, 256, 256)
        x = jax.random.normal(k1, (B, N, F), dtype=jnp.float32)
        adj = jax.random.uniform(k2, (B, N, N), dtype=jnp.float32)
        W = jax.random.normal(k3, (O, 2 * F), dtype=jnp.float32) * (1.0 / np.sqrt(2 * F))
        return {'x': x, 'adj': adj, 'W': W}
    _L3_gnn_all = _L3_gnn_setup()
    _L3_gnn_in = {k: v for k, v in _L3_gnn_all.items() if k in ('W',)}
    del _L3_gnn_all
    return {'x': x, 'adj': adj, 'L0_gnn_Wq_w': _L0_gnn_in['Wq_w'], 'L0_gnn_Wq_b': _L0_gnn_in['Wq_b'], 'L0_gnn_Wk_w': _L0_gnn_in['Wk_w'], 'L0_gnn_Wk_b': _L0_gnn_in['Wk_b'], 'L0_gnn_Wv_w': _L0_gnn_in['Wv_w'], 'L0_gnn_Wv_b': _L0_gnn_in['Wv_b'], 'L1_gnn_Wv': _L1_gnn_in['Wv'], 'L1_gnn_bv': _L1_gnn_in['bv'], 'L1_gnn_aw': _L1_gnn_in['aw'], 'L1_gnn_ab': _L1_gnn_in['ab'], 'L1_gnn_Wk': _L1_gnn_in['Wk'], 'L1_gnn_bk': _L1_gnn_in['bk'], 'L2_gnn_W1': _L2_gnn_in['W1'], 'L2_gnn_b1': _L2_gnn_in['b1'], 'L2_gnn_gamma': _L2_gnn_in['gamma'], 'L2_gnn_beta': _L2_gnn_in['beta'], 'L2_gnn_W2': _L2_gnn_in['W2'], 'L2_gnn_b2': _L2_gnn_in['b2'], 'L3_gnn_W': _L3_gnn_in['W']}

def reference(x, adj, L0_gnn_Wq_w, L0_gnn_Wq_b, L0_gnn_Wk_w, L0_gnn_Wk_b, L0_gnn_Wv_w, L0_gnn_Wv_b, L1_gnn_Wv, L1_gnn_bv, L1_gnn_aw, L1_gnn_ab, L1_gnn_Wk, L1_gnn_bk, L2_gnn_W1, L2_gnn_b1, L2_gnn_gamma, L2_gnn_beta, L2_gnn_W2, L2_gnn_b2, L3_gnn_W):
    import jax
    import jax.numpy as jnp

    def _L0_gnn_ref(x, adj, Wq_w, Wq_b, Wk_w, Wk_b, Wv_w, Wv_b):
        import jax, jax.numpy as jnp
        import numpy as np
        B, N, D = (8, 1024, 256)
        query = jnp.einsum('bnd,od->bno', x, Wq_w) + Wq_b
        keyt = jnp.einsum('bnd,od->bno', x, Wk_w) + Wk_b
        value = jnp.einsum('bnd,od->bno', x, Wv_w) + Wv_b
        weight = jnp.einsum('bqd,bkd->bqk', query, keyt)
        weight = adj * jnp.exp(weight)
        weight = weight / jnp.sum(weight, axis=2, keepdims=True)
        return jnp.einsum('bqk,bkd->bqd', weight, value)

    def _L1_gnn_ref(X, A, Wv, bv, aw, ab, Wk, bk):
        import jax, jax.numpy as jnp
        import numpy as np
        B, N, DIN, DOUT, K = (4, 1024, 256, 256, 3)
        d = Wv.shape[1]
        Xw = X @ Wv + bv
        sj = Xw @ aw[:d, 0]
        si = Xw @ aw[d:, 0]
        e = jax.nn.leaky_relu(sj[:, None, :] + si[:, :, None] + ab[0], negative_slope=0.2)
        alpha_matrix = A * jnp.exp(e)
        transition = alpha_matrix / (jnp.sum(alpha_matrix, axis=-1, keepdims=True) + 1e-12)
        H = jnp.zeros(X.shape[:-1] + (d,), dtype=X.dtype)
        Xk = X
        for k in range(Wk.shape[0]):
            H = H + Xk @ Wk[k] + bk[k]
            Xk = jnp.einsum('bij,bjd->bid', transition, Xk)
        return jax.nn.relu(H)

    def _L2_gnn_ref(x, adj, W1, b1, gamma, beta, W2, b2):
        import jax, jax.numpy as jnp
        import numpy as np
        EPS_LN = 1e-05

        def hypergraph_conv(x, adj, W, b):
            N, C, _ = adj.shape
            H = (adj != 0).astype(x.dtype)
            w = adj.reshape(N, -1)[:, :C]
            xw = jnp.einsum('ncd,hd->nch', x, W)
            Dn = jnp.einsum('nce,ne->nc', H, w)
            Dn = jnp.where(Dn > 0, 1.0 / Dn, 0.0)
            Be = H.sum(axis=1)
            Be = jnp.where(Be > 0, 1.0 / Be, 0.0)
            m = Be[:, :, None] * jnp.einsum('nce,nch->neh', H, xw)
            out = Dn[:, :, None] * jnp.einsum('nce,neh->nch', H, m)
            return out + b

        def layer_norm(x, g, b):
            mu = jnp.mean(x, axis=-1, keepdims=True)
            var = jnp.var(x, axis=-1, keepdims=True)
            return (x - mu) * jax.lax.rsqrt(var + EPS_LN) * g + b
        h = jax.nn.relu(hypergraph_conv(x, adj, W1, b1))
        h = layer_norm(h, gamma, beta)
        y = hypergraph_conv(h, adj, W2, b2)
        return y + x

    def _L3_gnn_ref(x, adj, W):
        import jax, jax.numpy as jnp
        import numpy as np
        EPS = 1e-06
        deg = jnp.sum(adj, axis=-1, keepdims=True)
        agg = jnp.einsum('bij,bjf->bif', adj, x) / jnp.maximum(deg, EPS)
        cat = jnp.concatenate([x, agg], axis=2)
        out = jnp.einsum('bnf,of->bno', cat, W)
        return jax.nn.relu(out)
    x = _layernorm(x + _L0_gnn_ref(x, adj, L0_gnn_Wq_w, L0_gnn_Wq_b, L0_gnn_Wk_w, L0_gnn_Wk_b, L0_gnn_Wv_w, L0_gnn_Wv_b), axis=-1)
    x = _layernorm(x + _L1_gnn_ref(x, adj, L1_gnn_Wv, L1_gnn_bv, L1_gnn_aw, L1_gnn_ab, L1_gnn_Wk, L1_gnn_bk), axis=-1)
    x = _layernorm(x + _L2_gnn_ref(x, adj, L2_gnn_W1, L2_gnn_b1, L2_gnn_gamma, L2_gnn_beta, L2_gnn_W2, L2_gnn_b2), axis=-1)
    x = _layernorm(x + _L3_gnn_ref(x, adj, L3_gnn_W), axis=-1)
    return x

_drawn_inputs = setup_inputs


def setup_inputs(seed=0):
    import zlib

    import numpy as np

    out = dict(_drawn_inputs(seed))
    spreads = {'L0_gnn_Wq_b': (0.0, 0.1),
     'L0_gnn_Wk_b': (0.0, 0.8),
     'L0_gnn_Wv_b': (0.0, 0.1),
     'L2_gnn_b1': (0.0, 0.1),
     'L2_gnn_gamma': (1.0, 0.2),
     'L2_gnn_beta': (0.0, 0.1),
     'L2_gnn_b2': (0.0, 0.1)}
    factors = {'L1_gnn_Wv': 2.875, 'L1_gnn_bv': 8.0, 'L1_gnn_aw': 2.988}
    for name, (base, spread) in spreads.items():
        noise = np.random.default_rng([zlib.crc32(name.encode()), seed]).standard_normal(out[name].shape)
        drawn = base * np.exp(spread * noise) if base else spread * noise
        out[name] = jnp.asarray(drawn.astype(out[name].dtype))
    for name, factor in factors.items():
        out[name] = (out[name] * factor).astype(out[name].dtype)
    return out
```

```python
from contextlib import ExitStack

import concourse.bass as bass
from concourse import mybir

F32 = mybir.dt.float32
F32R = mybir.dt.float32r
ALU = mybir.AluOpType
ACT = mybir.ActivationFunctionType

P = 128
LN_EPS = 1e-5
TINY = 1.2e-38


def build_graph_stack(nc, A):
    B, N, D = A["x"].shape
    DH = A["W1T"].shape[1]
    K = A["Wk"].shape[0]
    NT = N // P
    DT = D // P
    HT_ = DH // P
    G = 4
    assert NT == 2 and DT == 2 and N == D == 256 and B % G == 0 and K == 3

    ctx = ExitStack()
    with ctx:
        def sb(name, shape, dt=F32):
            return ctx.enter_context(nc.sbuf_tensor(name, shape, dt))

        def sem(name):
            return ctx.enter_context(nc.semaphore(name))

        def per_slot(name, shape, dt=F32):
            return [sb(f"{name}{g}", shape, dt) for g in range(G)]

        qk_hi, qk_lo = sb("qk_hi", [P, DT, D], F32R), sb("qk_lo", [P, DT, D], F32R)
        v_hi, v_lo = sb("v_hi", [P, DT, D], F32R), sb("v_lo", [P, DT, D], F32R)
        wk_hi, wk_lo = sb("wk_hi", [P, DT, K, D], F32R), sb("wk_lo", [P, DT, K, D], F32R)
        w1_hi, w1_lo = sb("w1_hi", [P, DT, DH], F32R), sb("w1_lo", [P, DT, DH], F32R)
        w3_hi, w3_lo = sb("w3_hi", [P, 2 * DT, D], F32R), sb("w3_lo", [P, 2 * DT, D], F32R)
        si_hi, si_lo = sb("si_hi", [P, DT, P], F32R), sb("si_lo", [P, DT, P], F32R)
        row_rep = sb("row_rep", [P, DT, P], F32R)
        w2c = sb("w2c", [P, HT_, D + 1])
        ident = sb("ident", [P, P])
        ones = sb("ones", [P, P])
        bv_bc = sb("bv_bc", [P, D])
        bk_bc = sb("bk_bc", [P, D])
        sj_bc = sb("sj_bc", [P, D])
        w2b_bc = sb("w2b_bc", [P, D])
        b2_bc = sb("b2_bc", [P, D])
        b1_col = sb("b1_col", [P, HT_])
        qk_col = sb("qk_col", [P, DT])
        bqbk = sb("bqbk", [P, 1])
        e_const = sb("e_const", [P, 1])
        cols = sb("cols", [P, 24])
        minus_half = sb("minus_half", [P, 2])
        eps_col = sb("eps_col", [P, 2])

        x = per_slot("x", [P, NT, D])
        xT = per_slot("xT", [P, DT, N])
        adj = per_slot("adj", [P, NT, N])
        adjT = per_slot("adjT", [P, NT, N])
        w_bc = per_slot("w_bc", [P, N])
        RA = per_slot("RA", [P, 2, 2, 256], F32R)
        RB = per_slot("RB", [P, 2, 2, 256], F32R)
        H = per_slot("H", [P, NT, N], F32R)
        HT = per_slot("HT", [P, NT, N], F32R)
        F = per_slot("F", [P, 4, 256])
        Y = per_slot("Y", [P, NT, D + 1])
        R4 = per_slot("R4", [P, 4, 256])
        X = per_slot("X", [P, NT, D])
        sm = per_slot("sm", [P, 64])
        ps = [ctx.enter_context(nc.psum_tensor(f"ps{g}", [P, 2, 512], F32)) for g in range(G)]

        def stats(g, t):
            return sm[g][:, 6 * t:6 * t + 6]

        def mv(g):
            return sm[g][:, 12:16].rearrange("p (t c) -> p t c", c=2)

        def rstd(g):
            return sm[g][:, 16:18]

        def rinv(g):
            return sm[g][:, 18:20]

        def rsum(g):
            return sm[g][:, 20:22]

        def sj(g):
            return sm[g][:, 22:24]

        def deg(g):
            return sm[g][:, 24:28]

        def deg_mask(g):
            return sm[g][:, 28:32]

        def deg_safe(g):
            return sm[g][:, 32:36]

        def deg_inv(g):
            return sm[g][:, 36:40]

        def hstat(g):
            return sm[g][:, 40:44].rearrange("p (t c) -> p t c", c=2)

        def hmean2(g):
            return sm[g][:, 44:46]

        def hvar(g):
            return sm[g][:, 46:48]

        def veps(g):
            return sm[g][:, 48:50]

        def sjraw(g):
            return sm[g][:, 50:52]

        def bank(g, b):
            return ps[g][:, b, :].rearrange("p (t n) -> p t n", t=2)

        ld_xT = [sem(f"ld_xT{g}") for g in range(G)]
        ld_x = [sem(f"ld_x{g}") for g in range(G)]
        ld_adj = [sem(f"ld_adj{g}") for g in range(G)]
        ld_adjT = [sem(f"ld_adjT{g}") for g in range(G)]
        ld_w = [sem(f"ld_w{g}") for g in range(G)]
        stored = [sem(f"stored{g}") for g in range(G)]
        names = """xT_hi xT_lo xb t_ps t_hi t_lo sT_ps v_ps eT v_sb pT pv_ps inv0 z0 st0 mv0 ve0 rs0 x1
            x1T_ps x1T_hi x1T_lo sjr sjc y2_ps y2 si_ps zs lk e1 T y1_ps y0_ps y1 y0 z1_ps den1 inv1 w1
            z2_ps h1 z1n st1 mv1 ve1 rs1 x2 Hs HTs dn dmask dsafe drec dinv diag
            x2_hi x2_lo x2b m_ps db_ps m_hi m_lo dbc uT_ps u u_hi u_lo h_ps r sq sqa sqs y_ps ss_ps
            hst hm2 hv ve2 rs2 yf yf_hi yf_lo m2_ps m2_hi m2_lo u2_ps z2n st3 mv3 ve3 rs3 x3
            x3T_ps x3T_hi x3T_lo yb_ps yb ya_ps ya ag_ps den4 inv4 banks_free z4 st4 mv4 ve4 rs4 outp""".split()
        s = {name: sem(name) for name in names}
        ld_wt = sem("ld_wt")
        p_const, p_id, p_rep, p_mm, p_ev, p_split = (
            sem("p_const"), sem("p_id"), sem("p_rep"), sem("p_mm"), sem("p_ev"), sem("p_split"))
        p_done = sem("p_done")
        stats_seen = sem("stats_seen")

        st_wq, st_wk = R4[0][:, 0:2, :], R4[0][:, 2:4, :]
        st_vT = R4[1][:, 0:2, :]
        st_aVT = R4[1][:, 2:4, :]
        st_kw = [R4[2][:, 0:2, :], R4[2][:, 2:4, :], R4[3][:, 0:2, :]]
        st_w1 = F[0][:, :, :].rearrange("p (k a) n -> p k (a n)", k=DT)
        st_w2 = F[1]
        st_w3 = F[2]
        st_bk3 = F[3][:, 0:3, :]
        bq_col, bk_col = cols[:, 0:2], cols[:, 2:4]
        awj_col, awi_col = cols[:, 4:6], cols[:, 6:8]
        abv_col = cols[:, 8:10]
        gam_col, bet_col = cols[:, 10:14], cols[:, 14:18]
        ab_col = cols[:, 18:19]
        aw_sum = cols[:, 20:22]
        rep_bk = X[0][:, :, 0:P]
        rep_awj = X[1][:, :, 0:P]
        rep_awi = X[2][:, :, 0:P]
        rep_aws = X[3][:, :, 0:P]
        rep_bet = Y[0][:, :, 0:256].rearrange("p t (a n) -> p t a n", a=2)

        n_weight_loads = 21
        block = ctx.enter_context(nc.Block())

        @block.sync
        def _(sp):
            def tiles(ap):
                return ap.rearrange("(t p) n -> p t n", p=P)

            def column(ap, k):
                return ap.rearrange("(t p) -> p t", p=P)[:, 0:k]

            for g in range(G):
                sp.sem_inc(stored[g], 16)

            def load(dst, src, sems, g):
                sp.dma_start(dst[g][:, :, :], src).then_inc(sems[g], 16)

            with nc.allow_non_contiguous_dma(reason="weight vectors as columns, once"):
                for dst, src in (
                    (st_wq, tiles(A["Wq"])), (st_wk, tiles(A["Wkey"])),
                    (bq_col, column(A["bq"], DT)), (bk_col, column(A["bkey"], DT)),
                    (st_aVT, tiles(A["aVT"])),
                    (awj_col, column(A["aw"][0:D], DT)), (awi_col, column(A["aw"][D:2 * D], DT)),
                    (abv_col, column(A["abv"], DT)),
                    (ab_col, A["ab"].partition_broadcast(P)),
                    (st_vT, tiles(A["WvT"])),
                    (bv_bc[:, :], A["bv"].partition_broadcast(P)),
                    (st_kw[0], tiles(A["Wk"][0])), (st_kw[1], tiles(A["Wk"][1])),
                    (st_kw[2], tiles(A["Wk"][2])),
                    (st_bk3, A["bk"].partition_broadcast(P)),
                    (st_w1, tiles(A["W1T"])), (b1_col[:, :], column(A["b1"], HT_)),
                    (gam_col, column(A["gamma"], HT_)), (bet_col, column(A["beta"], HT_)),
                    (st_w2[:, :, :], tiles(A["W2T"])),
                    (st_w3[:, :, :], tiles(A["W3T"])),
                ):
                    sp.dma_start(dst, src).then_inc(ld_wt, 16)
                sp.dma_start(b2_bc[:, :], A["b2"].partition_broadcast(P)).then_inc(ld_wt, 16)
            for g in range(G):
                load(xT, tiles(A["xT"][g]), ld_xT, g)
                load(adjT, tiles(A["adjT"][g]), ld_adjT, g)
                load(x, tiles(A["x"][g]), ld_x, g)
                load(adj, tiles(A["adj"][g]), ld_adj, g)
                sp.dma_start(w_bc[g][:, :], A["adj"][g][0:1, :].rearrange("a n -> (a n)").partition_broadcast(P)).then_inc(ld_w[g], 16)

            def view(name, j, g):
                slot = A[name].rearrange("(j g) r n -> g j r n", g=G)[g]
                return slot[bass.ds(j, 1), :, :].rearrange("a (t p) n -> p (a t) n", p=P)

            with sp.Fori(0, B // G - 1, 1) as j:
                n = [sp.snap(j * G + (g + 1)) for g in range(G)]
                for g in range(G):
                    sp.wait_ge(s["xT_lo"], n[g])
                    load(xT, view("xT", j + 1, g), ld_xT, g)
                for g in range(G):
                    sp.wait_ge(s["z0"], n[g])
                    load(x, view("x", j + 1, g), ld_x, g)
                for g in range(G):
                    sp.wait_ge(s["dn"], n[g])
                    load(adj, view("adj", j + 1, g), ld_adj, g)
                for g in range(G):
                    sp.wait_ge(s["db_ps"], n[g])
                    src = A["adj"].rearrange("(j g) r n -> g j r n", g=G)[g, bass.ds(j + 1, 1), 0, :].rearrange("a n -> (a n)")
                    sp.dma_start(w_bc[g][:, :], src.partition_broadcast(P)).then_inc(ld_w[g], 16)
                for g in range(G):
                    sp.wait_ge(s["ag_ps"], n[g])
                    load(adjT, view("adjT", j + 1, g), ld_adjT, g)
                for g in range(G):
                    sp.wait_ge(s["outp"], n[g])
                    sp.dma_start(view("out", j, g), R4[g][:, 2:4, :]).then_inc(stored[g], 16)
            for g in range(G):
                sp.wait_ge(s["outp"], B - G + g + 1)
                sp.dma_start(tiles(A["out"][B - G + g]), R4[g][:, 2:4, :]).then_inc(stored[g], 16)
            for g in range(G):
                sp.wait_ge(stored[g], 16 * (B // G + 1))

        @block.gpsimd
        def _(pool):
            pool.memset(ident[:, :], 0.0).then_inc(p_id, 1)
            pool.memset(ones[:, :], 1.0)
            pool.memset(eps_col[:, :], LN_EPS)
            pool.memset(minus_half[:, :], -0.5).then_inc(p_const, 1)
            pool.wait_ge(p_id, 1)
            pool.affine_select(out=ident[:, :], in_=ident[:, :], compare_op=ALU.not_equal, fill=1.0,
                               base=0, pattern=[[-1, P]], channel_multiplier=1).then_inc(p_id, 1)
            pool.wait_ge(p_id, 2)
            pool.wait_ge(p_const, 1)

            def rsqrt(var, raised, done, n, g):
                pool.tensor_tensor(veps(g), var, eps_col[:, :], ALU.add).then_inc(s[raised], 1)
                pool.wait_ge(s[raised], n)
                pool.tensor_tensor(rstd(g), veps(g), minus_half[:, :], ALU.pow).then_inc(s[done], 1)

            pool.wait_ge(p_done, 1)
            with pool.Fori(0, B, G) as i:
                n = [pool.snap(i + (g + 1)) for g in range(G)]
                l16 = pool.snap(i * (16 // G) + 16)
                for g in range(G):
                    pool.wait_ge(s["xT_hi"], n[g])
                    pool.tensor_tensor(RA[g][:, 1], xT[g][:, :, :], RA[g][:, 0].bitcast(F32),
                                       ALU.subtract).then_inc(s["xT_lo"], 1)
                for g in range(G):
                    pool.wait_ge(ld_x[g], l16)
                    pool.tensor_tensor(x[g][:, :, :], x[g][:, :, :],
                                       bv_bc[:, None, :].to_broadcast([P, NT, D]), ALU.add).then_inc(s["xb"], 1)
                for g in range(G):
                    pool.wait_ge(s["eT"], n[g])
                    pool.wait_ge(ld_adjT[g], l16)
                    pool.tensor_tensor(F[g][:, 0:2, :], F[g][:, 0:2, :], adjT[g][:, :, :],
                                       ALU.mult).then_inc(s["pT"], 1)
                for g in range(G):
                    pool.wait_ge(s["mv0"], n[g])
                    rsqrt(mv(g)[:, :, 1], "ve0", "rs0", n[g], g)
                for g in range(G):
                    pool.wait_ge(s["dinv"], n[g])
                    for t in range(NT):
                        last = pool.tensor_tensor(w_bc[g][:, t * P:(t + 1) * P], ident[:, :],
                                                  deg_inv(g)[:, t:t + 1].to_broadcast([P, P]), ALU.mult)
                    last.then_inc(s["diag"], 1)
                for g in range(G):
                    pool.wait_ge(s["e1"], n[g])
                    pool.tensor_tensor(F[g][:, 0:2, :], F[g][:, 0:2, :], adjT[g][:, :, :],
                                       ALU.mult).then_inc(s["T"], 1)
                for g in range(G):
                    pool.wait_ge(s["mv1"], n[g])
                    rsqrt(mv(g)[:, :, 1], "ve1", "rs1", n[g], g)
                for g in range(G):
                    pool.wait_ge(s["x2_hi"], n[g])
                    pool.tensor_tensor(RB[g][:, 1], X[g][:, :, :], RB[g][:, 0].bitcast(F32),
                                       ALU.subtract).then_inc(s["x2_lo"], 1)
                for g in range(G):
                    pool.wait_ge(s["u_hi"], n[g])
                    pool.tensor_tensor(RB[g][:, 1], F[g][:, 0:2, :], RB[g][:, 0].bitcast(F32),
                                       ALU.subtract).then_inc(s["u_lo"], 1)
                for g in range(G):
                    pool.wait_ge(s["hv"], n[g])
                    rsqrt(hvar(g), "ve2", "rs2", n[g], g)
                for g in range(G):
                    pool.wait_ge(s["yf_hi"], n[g])
                    pool.tensor_tensor(RA[g][:, 1], Y[g][:, :, 0:D], RA[g][:, 0].bitcast(F32),
                                       ALU.subtract).then_inc(s["yf_lo"], 1)
                for g in range(G):
                    pool.wait_ge(s["mv3"], n[g])
                    rsqrt(mv(g)[:, :, 1], "ve3", "rs3", n[g], g)
                for g in range(G):
                    pool.wait_ge(s["mv4"], n[g])
                    rsqrt(mv(g)[:, :, 1], "ve4", "rs4", n[g], g)

        @block.scalar
        def _(act):
            act.wait_ge(p_done, 1)
            with act.Fori(0, B, G) as i:
                n = [act.snap(i + (g + 1)) for g in range(G)]
                l16 = act.snap(i * (16 // G) + 16)
                for g in range(G):
                    act.wait_ge(ld_xT[g], l16)
                    act.activation(RA[g][:, 0], xT[g][:, :, :], ACT.Copy).then_inc(s["xT_hi"], 1)
                for g in range(G):
                    act.wait_ge(s["t_ps"], n[g])
                    for d in range(DT):
                        last = act.activation(RB[g][:, 0, d], bank(g, 0)[:, d], ACT.Identity,
                                              bias=qk_col[:, d:d + 1])
                    last.then_inc(s["t_hi"], 1)
                for g in range(G):
                    act.wait_ge(s["sT_ps"], n[g])
                    act.activation(F[g][:, 0:2, :], bank(g, 1), ACT.Exp, bias=bqbk[:, 0:1]).then_inc(s["eT"], 1)
                    act.wait_ge(s["v_ps"], n[g])
                    act.activation(Y[g][:, :, 0:D], bank(g, 0), ACT.Copy).then_inc(s["v_sb"], 1)
                for g in range(G):
                    act.wait_ge(s["x1T_ps"], n[g])
                    act.activation(RA[g][:, 0], bank(g, 0), ACT.Copy).then_inc(s["x1T_hi"], 1)
                for g in range(G):
                    act.wait_ge(s["y2_ps"], n[g])
                    act.activation(Y[g][:, :, 0:D], bank(g, 1), ACT.Copy).then_inc(s["y2"], 1)
                    act.wait_ge(s["si_ps"], n[g])
                    act.wait_ge(s["sjc"], n[g])
                    for t in range(NT):
                        last = act.activation(F[g][:, t, :], bank(g, 0)[:, 0], ACT.Identity,
                                              bias=sj(g)[:, t:t + 1])
                    last.then_inc(s["zs"], 1)
                for g in range(G):
                    act.wait_ge(s["lk"], n[g])
                    act.activation(F[g][:, 0:2, :], F[g][:, 2:4, :], ACT.Exp).then_inc(s["e1"], 1)
                    act.wait_ge(s["y1_ps"], n[g])
                    act.activation(R4[g][:, 0:2, :], bank(g, 1), ACT.Copy).then_inc(s["y1"], 1)
                for g in range(G):
                    act.wait_ge(s["x2"], n[g])
                    act.activation(RB[g][:, 0], X[g][:, :, :], ACT.Copy).then_inc(s["x2_hi"], 1)
                for g in range(G):
                    act.wait_ge(s["m_ps"], n[g])
                    for t in range(NT):
                        last = act.activation(RA[g][:, 0, t], bank(g, 1)[:, t], ACT.Copy,
                                              scale=deg_inv(g)[:, 2 + t:3 + t])
                    last.then_inc(s["m_hi"], 1)
                    act.wait_ge(s["db_ps"], n[g])
                    act.activation(Y[g][:, 0, 0:D], bank(g, 0)[:, 0], ACT.Copy).then_inc(s["dbc"], 1)
                for g in range(G):
                    act.wait_ge(s["u"], n[g])
                    act.activation(RB[g][:, 0], F[g][:, 0:2, :], ACT.Copy).then_inc(s["u_hi"], 1)
                for g in range(G):
                    act.wait_ge(s["h_ps"], n[g])
                    for k in range(HT_):
                        last = act.activation(R4[g][:, k, :], bank(g, k // 2)[:, k % 2], ACT.Relu,
                                              bias=b1_col[:, k:k + 1])
                    last.then_inc(s["r"], 1)
                    act.wait_ge(s["r"], n[g])
                    act.wait_ge(s["u_lo"], n[g])
                    act.activation(F[g][:, :, :], R4[g][:, :, :], ACT.Square).then_inc(s["sq"], 1)
                for g in range(G):
                    act.wait_ge(s["yf"], n[g])
                    act.activation(RA[g][:, 0], Y[g][:, :, 0:D], ACT.Copy).then_inc(s["yf_hi"], 1)
                for g in range(G):
                    act.wait_ge(s["m2_ps"], n[g])
                    for t in range(NT):
                        last = act.activation(RB[g][:, 0, t], bank(g, 0)[:, t], ACT.Copy,
                                              scale=deg_inv(g)[:, 2 + t:3 + t])
                    last.then_inc(s["m2_hi"], 1)
                for g in range(G):
                    act.wait_ge(s["x3T_ps"], n[g])
                    act.activation(RA[g][:, 0], bank(g, 0), ACT.Copy).then_inc(s["x3T_hi"], 1)
                for g in range(G):
                    act.wait_ge(s["yb_ps"], n[g])
                    act.activation(Y[g][:, :, 0:D], bank(g, 1), ACT.Copy).then_inc(s["yb"], 1)
                    act.wait_ge(s["ya_ps"], n[g])
                    act.activation(R4[g][:, 0:2, :], bank(g, 0), ACT.Copy).then_inc(s["ya"], 1)

        @block.vector
        def _(dve):
            ev = [0]

            def step(ins):
                ins.then_inc(p_ev, 1)
                ev[0] += 1
                dve.wait_ge(p_ev, ev[0])

            dve.sem_inc(s["banks_free"], G)
            dve.wait_ge(ld_wt, 16 * (n_weight_loads + 1))
            dve.wait_ge(p_const, 1)
            step(dve.tensor_tensor(aw_sum, awj_col, awi_col, ALU.add))
            for t in range(2):
                for rep, col in ((rep_bk, bk_col), (rep_awj, awj_col), (rep_awi, awi_col), (rep_aws, aw_sum)):
                    dve.tensor_scalar(rep[:, t, :], ones[:, :], col[:, t:t + 1], None, ALU.mult)
            for k in range(HT_):
                dve.tensor_scalar(rep_bet[:, k // 2, k % 2, :], ones[:, :], bet_col[:, k:k + 1], None, ALU.mult)
                last = dve.tensor_scalar(w2c[:, k, 0:D], st_w2[:, k, :], gam_col[:, k:k + 1], None, ALU.mult)
            last.then_inc(p_rep, 1)
            pairs = [(v_hi[:, :, :], v_lo[:, :, :], st_vT), (w1_hi[:, :, :], w1_lo[:, :, :], st_w1),
                     (w3_hi[:, :, :], w3_lo[:, :, :], st_w3[:, :, :])]
            pairs += [(wk_hi[:, :, k, :], wk_lo[:, :, k, :], st_kw[k]) for k in range(K)]
            for hi, lo, full in pairs:
                last = dve.tensor_copy(hi, full)
            step(last)
            for hi, lo, full in pairs:
                dve.tensor_tensor(lo, full, hi.bitcast(F32), ALU.subtract)
            step(dve.tensor_tensor(bk_bc[:, :], st_bk3[:, 0, :], st_bk3[:, 1, :], ALU.add))
            step(dve.tensor_tensor(bk_bc[:, :], bk_bc[:, :], st_bk3[:, 2, :], ALU.add))
            dve.wait_ge(p_mm, 1)
            dve.tensor_copy(qk_hi[:, :, :], bank(0, 0))
            dve.tensor_copy(si_hi[:, :, :], bank(1, 0)[:, :, 0:P])
            dve.tensor_copy(row_rep[:, :, :], bank(1, 1)[:, :, 0:P])
            dve.tensor_copy(sj_bc[:, :], bank(2, 0)[:, 0])
            dve.tensor_copy(w2b_bc[:, :], bank(2, 1)[:, 0])
            dve.tensor_copy(qk_col[:, :], ps[3][:, 0, 0:2])
            dve.tensor_copy(bqbk[:, :], ps[3][:, 0, 2:3])
            step(dve.tensor_tensor(e_const[:, :], ps[3][:, 0, 3:4], ab_col, ALU.add))
            dve.tensor_tensor(qk_lo[:, :, :], bank(0, 0), qk_hi[:, :, :].bitcast(F32), ALU.subtract)
            dve.tensor_tensor(si_lo[:, :, :], bank(1, 0)[:, :, 0:P], si_hi[:, :, :].bitcast(F32), ALU.subtract)
            for k in range(HT_):
                dve.scalar_tensor_tensor(w2c[:, k, 0:D], ps[3][:, 1, 0:D], -1.0 / DH, w2c[:, k, 0:D],
                                         ALU.mult, ALU.add)
            dve.memset(w2c[:, :, D:D + 1], 1.0)
            for g in range(G):
                last = dve.memset(Y[g][:, :, D:D + 1], 1.0)
            last.then_inc(p_done, 1)
            dve.wait_ge(p_done, 1)

            def layer_norm_stats(src, st, mvs, n, g):
                for t in range(NT):
                    last = dve.bn_stats(stats(g, t), src[:, t, :])
                last.then_inc(s[st], 1)
                dve.wait_ge(s[st], n)
                dve.sem_inc(stats_seen, 1)
                for t in range(NT):
                    last = dve.bn_aggr(mv(g)[:, t, :], stats(g, t))
                last.then_inc(s[mvs], 1)

            def normalise(dst, src, done, g):
                for t in range(NT):
                    last = dve.tensor_scalar(dst[:, t, :], src[:, t, :], mv(g)[:, t, 0:1], rstd(g)[:, t:t + 1],
                                             ALU.subtract, ALU.mult)
                last.then_inc(s[done], 1)

            with dve.Fori(0, B, G) as i:
                n = [dve.snap(i + (g + 1)) for g in range(G)]
                l16 = dve.snap(i * (16 // G) + 16)
                for g in range(G):
                    dve.wait_ge(s["t_hi"], n[g])
                    for d in range(DT):
                        last = dve.scalar_tensor_tensor(RB[g][:, 1, d], bank(g, 0)[:, d], qk_col[:, d:d + 1],
                                                        RB[g][:, 0, d].bitcast(F32), ALU.add, ALU.subtract)
                    last.then_inc(s["t_lo"], 1)
                for g in range(G):
                    dve.wait_ge(ld_adj[g], l16)
                    dve.tensor_scalar(H[g][:, :, :], adj[g][:, :, :], 0.0, None, ALU.not_equal)\
                       .then_inc(s["Hs"], 1)
                    dve.wait_ge(ld_adjT[g], l16)
                    for t in range(NT):
                        last = dve.tensor_scalar(HT[g][:, t, :], adjT[g][:, t, :], 0.0, None, ALU.not_equal,
                                                 ALU.add, accum_out=deg(g)[:, 2 + t:3 + t])
                    last.then_inc(s["HTs"], 1)
                    dve.wait_ge(ld_w[g], l16)
                    dve.wait_ge(s["Hs"], n[g])
                    for t in range(NT):
                        last = dve.scalar_tensor_tensor(adj[g][:, t, :], H[g][:, t, :].bitcast(F32), 1.0,
                                                        w_bc[g][:, :], ALU.mult, ALU.mult,
                                                        accum_out=deg(g)[:, t:t + 1])
                    last.then_inc(s["dn"], 1)
                    dve.wait_ge(s["HTs"], n[g])
                    dve.wait_ge(s["dn"], n[g])
                    dve.tensor_scalar(deg_mask(g), deg(g), 0.0, None, ALU.is_gt).then_inc(s["dmask"], 1)
                    dve.tensor_scalar(deg_safe(g), deg(g), TINY, None, ALU.max).then_inc(s["dsafe"], 1)
                    dve.wait_ge(s["dsafe"], n[g])
                    dve.reciprocal(deg_safe(g), deg_safe(g)).then_inc(s["drec"], 1)
                    dve.wait_ge(s["dmask"], n[g])
                    dve.wait_ge(s["drec"], n[g])
                    dve.tensor_tensor(deg_inv(g), deg_safe(g), deg_mask(g), ALU.mult).then_inc(s["dinv"], 1)
                for g in range(G):
                    dve.wait_ge(s["pv_ps"], n[g])
                    dve.reciprocal(rinv(g), ps[g][:, :, D]).then_inc(s["inv0"], 1)
                    dve.wait_ge(s["inv0"], n[g])
                    dve.wait_ge(s["xb"], n[g])
                    for t in range(NT):
                        last = dve.scalar_tensor_tensor(F[g][:, 2 + t, :], ps[g][:, t, 0:D], rinv(g)[:, t:t + 1],
                                                        x[g][:, t, :], ALU.mult, ALU.add)
                    last.then_inc(s["z0"], 1)
                    dve.wait_ge(s["z0"], n[g])
                    layer_norm_stats(F[g][:, 2:4, :], "st0", "mv0", n[g], g)
                for g in range(G):
                    dve.wait_ge(s["rs0"], n[g])
                    normalise(X[g], F[g][:, 2:4, :], "x1", g)
                for g in range(G):
                    dve.wait_ge(s["x1"], n[g])
                    for t in range(NT):
                        last = dve.scalar_tensor_tensor(F[g][:, 2 + t, :], X[g][:, t, :], 1.0, sj_bc[:, :],
                                                        ALU.mult, ALU.mult, accum_out=sjraw(g)[:, t:t + 1])
                    last.then_inc(s["sjr"], 1)
                    dve.wait_ge(s["sjr"], n[g])
                    dve.tensor_scalar(sj(g), sjraw(g), e_const[:, 0:1], None, ALU.add).then_inc(s["sjc"], 1)
                    dve.wait_ge(s["x1T_hi"], n[g])
                    dve.tensor_tensor(RA[g][:, 1], bank(g, 0), RA[g][:, 0].bitcast(F32), ALU.subtract)\
                       .then_inc(s["x1T_lo"], 1)
                for g in range(G):
                    dve.wait_ge(s["zs"], n[g])
                    dve.scalar_tensor_tensor(F[g][:, 2:4, :], F[g][:, 0:2, :], 0.2, F[g][:, 0:2, :],
                                             ALU.mult, ALU.max).then_inc(s["lk"], 1)
                for g in range(G):
                    dve.wait_ge(s["y0_ps"], n[g])
                    dve.wait_ge(stored[g], l16)
                    dve.tensor_tensor(R4[g][:, 2:4, :], bank(g, 0),
                                      bk_bc[:, None, :].to_broadcast([P, NT, D]), ALU.add).then_inc(s["y0"], 1)
                for g in range(G):
                    dve.wait_ge(s["z1_ps"], n[g])
                    dve.tensor_scalar(rsum(g), ps[g][:, :, D], 1e-12, None, ALU.add).then_inc(s["den1"], 1)
                    dve.wait_ge(s["den1"], n[g])
                    dve.reciprocal(rinv(g), rsum(g)).then_inc(s["inv1"], 1)
                    dve.wait_ge(s["inv1"], n[g])
                    for t in range(NT):
                        last = dve.scalar_tensor_tensor(R4[g][:, t, :], ps[g][:, t, 0:D], rinv(g)[:, t:t + 1],
                                                        R4[g][:, t, :], ALU.mult, ALU.add)
                    last.then_inc(s["w1"], 1)
                for g in range(G):
                    dve.wait_ge(s["z2_ps"], n[g])
                    for t in range(NT):
                        last = dve.scalar_tensor_tensor(F[g][:, 2 + t, :], bank(g, 0)[:, t], rinv(g)[:, t:t + 1],
                                                        R4[g][:, 2 + t, :], ALU.mult, ALU.add)
                    last.then_inc(s["h1"], 1)
                    dve.wait_ge(s["h1"], n[g])
                    dve.scalar_tensor_tensor(F[g][:, 0:2, :], F[g][:, 2:4, :], 0.0, X[g][:, :, :],
                                             ALU.max, ALU.add).then_inc(s["z1n"], 1)
                    dve.wait_ge(s["z1n"], n[g])
                    layer_norm_stats(F[g][:, 0:2, :], "st1", "mv1", n[g], g)
                for g in range(G):
                    dve.wait_ge(s["rs1"], n[g])
                    normalise(X[g], F[g][:, 0:2, :], "x2", g)
                for g in range(G):
                    dve.wait_ge(s["m_hi"], n[g])
                    for t in range(NT):
                        last = dve.scalar_tensor_tensor(RA[g][:, 1, t], bank(g, 1)[:, t], deg_inv(g)[:, 2 + t:3 + t],
                                                        RA[g][:, 0, t].bitcast(F32), ALU.mult, ALU.subtract)
                    last.then_inc(s["m_lo"], 1)
                    dve.wait_ge(s["x2_lo"], n[g])
                    dve.scalar_tensor_tensor(X[g][:, :, :], X[g][:, :, :], 2.0,
                                             b2_bc[:, None, :].to_broadcast([P, NT, D]), ALU.mult, ALU.add)\
                       .then_inc(s["x2b"], 1)
                for g in range(G):
                    dve.wait_ge(s["uT_ps"], n[g])
                    dve.wait_ge(s["dbc"], n[g])
                    dve.tensor_tensor(F[g][:, 0:2, :], bank(g, 1),
                                      Y[g][:, 0:1, 0:D].to_broadcast([P, 2, D]), ALU.mult).then_inc(s["u"], 1)
                for g in range(G):
                    dve.wait_ge(s["sq"], n[g])
                    dve.tensor_tensor(F[g][:, 0:2, :], F[g][:, 0:2, :], F[g][:, 2:4, :], ALU.add)\
                       .then_inc(s["sqa"], 1)
                    dve.wait_ge(s["sqa"], n[g])
                    dve.tensor_tensor(F[g][:, 2, :], F[g][:, 0, :], F[g][:, 1, :], ALU.add).then_inc(s["sqs"], 1)
                for g in range(G):
                    dve.wait_ge(s["ss_ps"], n[g])
                    dve.tensor_scalar(hstat(g), ps[g][:, :, D:D + 2], 1.0 / DH, None, ALU.mult)\
                       .then_inc(s["hst"], 1)
                    dve.wait_ge(s["hst"], n[g])
                    dve.tensor_tensor(hmean2(g), hstat(g)[:, :, 0], hstat(g)[:, :, 0], ALU.mult)\
                       .then_inc(s["hm2"], 1)
                    dve.wait_ge(s["hm2"], n[g])
                    dve.tensor_tensor(hvar(g), hstat(g)[:, :, 1], hmean2(g), ALU.subtract).then_inc(s["hv"], 1)
                for g in range(G):
                    dve.wait_ge(s["rs2"], n[g])
                    for t in range(NT):
                        last = dve.scalar_tensor_tensor(Y[g][:, t, 0:D], ps[g][:, t, 0:D], rstd(g)[:, t:t + 1],
                                                        w2b_bc[:, :], ALU.mult, ALU.add)
                    last.then_inc(s["yf"], 1)
                for g in range(G):
                    dve.wait_ge(s["m2_hi"], n[g])
                    for t in range(NT):
                        last = dve.scalar_tensor_tensor(RB[g][:, 1, t], bank(g, 0)[:, t], deg_inv(g)[:, 2 + t:3 + t],
                                                        RB[g][:, 0, t].bitcast(F32), ALU.mult, ALU.subtract)
                    last.then_inc(s["m2_lo"], 1)
                for g in range(G):
                    dve.wait_ge(s["u2_ps"], n[g])
                    dve.wait_ge(s["x2b"], n[g])
                    for t in range(NT):
                        last = dve.scalar_tensor_tensor(F[g][:, t, :], bank(g, 1)[:, t], deg_inv(g)[:, t:t + 1],
                                                        X[g][:, t, :], ALU.mult, ALU.add)
                    last.then_inc(s["z2n"], 1)
                    dve.wait_ge(s["z2n"], n[g])
                    layer_norm_stats(F[g][:, 0:2, :], "st3", "mv3", n[g], g)
                for g in range(G):
                    dve.wait_ge(s["rs3"], n[g])
                    normalise(X[g], F[g][:, 0:2, :], "x3", g)
                for g in range(G):
                    dve.wait_ge(s["x3T_hi"], n[g])
                    dve.tensor_tensor(RA[g][:, 1], bank(g, 0), RA[g][:, 0].bitcast(F32), ALU.subtract)\
                       .then_inc(s["x3T_lo"], 1)
                for g in range(G):
                    dve.wait_ge(s["ag_ps"], n[g])
                    dve.tensor_scalar(rsum(g), ps[g][:, :, D], 1e-6, None, ALU.max).then_inc(s["den4"], 1)
                    dve.wait_ge(s["den4"], n[g])
                    dve.reciprocal(rinv(g), rsum(g)).then_inc(s["inv4"], 1)
                    dve.wait_ge(s["inv4"], n[g])
                    for t in range(NT):
                        last = dve.scalar_tensor_tensor(F[g][:, t, :], ps[g][:, t, 0:D], rinv(g)[:, t:t + 1],
                                                        R4[g][:, t, :], ALU.mult, ALU.add)
                    last.then_inc(s["banks_free"], 1)
                    dve.wait_ge(s["banks_free"], n[g] + G)
                    dve.scalar_tensor_tensor(F[g][:, 2:4, :], F[g][:, 0:2, :], 0.0, X[g][:, :, :],
                                             ALU.max, ALU.add).then_inc(s["z4"], 1)
                    dve.wait_ge(s["z4"], n[g])
                    layer_norm_stats(F[g][:, 2:4, :], "st4", "mv4", n[g], g)
                for g in range(G):
                    dve.wait_ge(s["rs4"], n[g])
                    normalise(R4[g][:, 2:4, :], F[g][:, 2:4, :], "outp", g)

        @block.tensor
        def _(pe):
            def product(out, lhs, rhs, kt):
                for k in range(kt):
                    for n, (a, b) in enumerate(((0, 0), (0, 1), (1, 0))):
                        last = pe.matmul(out, lhs(k, a), rhs(k, b), start=(k == 0 and n == 0),
                                         stop=(k == kt - 1 and n == 2))
                return last

            def incidence_product(out, lhs, rhs, kt):
                for k in range(kt):
                    for b in range(2):
                        last = pe.matmul(out, lhs(k, b), rhs(k, b), start=(k == 0 and b == 0),
                                         stop=(k == kt - 1 and b == 1))
                return last

            def plain(out, lhs, rhs, kt):
                for k in range(kt):
                    last = pe.matmul(out, lhs(k), rhs(k), start=(k == 0), stop=(k == kt - 1))
                return last

            def tl(t):
                return slice(t * P, (t + 1) * P)

            pe.wait_ge(ld_wt, 16 * (n_weight_loads + 1))
            pe.wait_ge(p_rep, 1)
            pe.wait_ge(p_id, 2)
            for d in range(DT):
                plain(bank(0, 0)[:, d], lambda k: st_wq[:, k, tl(d)], lambda k: st_wk[:, k, :], DT)
                plain(bank(1, 0)[:, d, 0:P], lambda k: st_aVT[:, k, tl(d)], lambda k: rep_awi[:, k, :], DT)
                plain(bank(1, 1)[:, d, 0:P], lambda k: st_wq[:, k, tl(d)], lambda k: rep_bk[:, k, :], DT)
                plain(ps[3][:, 0, d:d + 1], lambda k: st_wk[:, k, tl(d)], lambda k: bq_col[:, k:k + 1], DT)
            plain(bank(2, 0)[:, 0], lambda k: rep_awj[:, k, :], lambda k: st_aVT[:, k, :], DT)
            plain(bank(2, 1)[:, 0], lambda k: rep_bet[:, k // 2, k % 2, :], lambda k: st_w2[:, k, :], HT_)
            plain(ps[3][:, 0, 2:3], lambda k: rep_bk[:, k, :], lambda k: bq_col[:, k:k + 1], DT)
            plain(ps[3][:, 0, 3:4], lambda k: rep_aws[:, k, :], lambda k: abv_col[:, k:k + 1], DT)
            plain(ps[3][:, 1, 0:D], lambda k: ones[:, :], lambda k: w2c[:, k, 0:D], HT_).then_inc(p_mm, 1)
            pe.wait_ge(p_done, 1)

            def transpose(src, g):
                for d in range(DT):
                    for t in range(NT):
                        last = pe.transpose(bank(g, 0)[:, d, tl(t)], src[:, t, tl(d)], ident[:, :])
                return last

            with pe.Fori(0, B, G) as i:
                n = [pe.snap(i + (g + 1)) for g in range(G)]
                for g in range(G):
                    pe.wait_ge(s["xT_lo"], n[g])
                    pe.wait_ge(s["banks_free"], n[g])
                    qk = (qk_hi, qk_lo)
                    for d in range(DT):
                        last = product(bank(g, 0)[:, d], lambda k, a: qk[a][:, k, tl(d)],
                                       lambda k, b: RA[g][:, b, k], DT)
                    last.then_inc(s["t_ps"], 1)
                for g in range(G):
                    pe.wait_ge(s["t_lo"], n[g])
                    for t in range(NT):
                        for k in range(DT):
                            pe.matmul(bank(g, 1)[:, t], row_rep[:, k, :], RA[g][:, 0, k], start=(k == 0), stop=False)
                        for k in range(DT):
                            for m, (a, b) in enumerate(((0, 0), (0, 1), (1, 0))):
                                last = pe.matmul(bank(g, 1)[:, t], RA[g][:, a, k, tl(t)], RB[g][:, b, k],
                                                 start=False, stop=(k == DT - 1 and m == 2))
                    last.then_inc(s["sT_ps"], 1)
                    vw = (v_hi, v_lo)
                    for t in range(NT):
                        last = product(bank(g, 0)[:, t], lambda k, a: RA[g][:, a, k, tl(t)],
                                       lambda k, b: vw[b][:, k, :], DT)
                    last.then_inc(s["v_ps"], 1)
                for g in range(G):
                    pe.wait_ge(s["pT"], n[g])
                    pe.wait_ge(s["v_sb"], n[g])
                    for t in range(NT):
                        last = plain(ps[g][:, t, 0:D + 1], lambda k: F[g][:, k, tl(t)], lambda k: Y[g][:, k, :], NT)
                    last.then_inc(s["pv_ps"], 1)
                for g in range(G):
                    pe.wait_ge(s["x1"], n[g])
                    transpose(X[g], g).then_inc(s["x1T_ps"], 1)

                def project(g, b, kk):
                    wk = (wk_hi, wk_lo)
                    for t in range(NT):
                        last = product(bank(g, b)[:, t], lambda k, a: RA[g][:, a, k, tl(t)],
                                       lambda k, c: wk[c][:, k, kk, :], DT)
                    return last

                for g in range(G):
                    pe.wait_ge(s["x1T_lo"], n[g])
                    project(g, 1, 2).then_inc(s["y2_ps"], 1)
                    si = (si_hi, si_lo)
                    product(bank(g, 0)[:, 0], lambda k, a: si[a][:, k, :], lambda k, b: RA[g][:, b, k], DT)\
                        .then_inc(s["si_ps"], 1)
                for g in range(G):
                    pe.wait_ge(s["y2"], n[g])
                    project(g, 1, 1).then_inc(s["y1_ps"], 1)
                    pe.wait_ge(s["zs"], n[g])
                    project(g, 0, 0).then_inc(s["y0_ps"], 1)
                for g in range(G):
                    pe.wait_ge(s["T"], n[g])
                    pe.wait_ge(s["y1"], n[g])
                    pe.wait_ge(s["y0"], n[g])
                    for t in range(NT):
                        last = plain(ps[g][:, t, 0:D + 1], lambda k: F[g][:, k, tl(t)], lambda k: Y[g][:, k, :], NT)
                    last.then_inc(s["z1_ps"], 1)
                for g in range(G):
                    pe.wait_ge(s["w1"], n[g])
                    for t in range(NT):
                        last = plain(bank(g, 0)[:, t], lambda k: F[g][:, k, tl(t)], lambda k: R4[g][:, k, :], NT)
                    last.then_inc(s["z2_ps"], 1)
                for g in range(G):
                    pe.wait_ge(s["x2_lo"], n[g])
                    pe.wait_ge(s["Hs"], n[g])
                    for t in range(NT):
                        last = incidence_product(bank(g, 1)[:, t], lambda k, b: H[g][:, k, tl(t)],
                                                 lambda k, b: RB[g][:, b, k], NT)
                    last.then_inc(s["m_ps"], 1)
                    pe.wait_ge(s["diag"], n[g])
                    for t in range(NT):
                        last = pe.matmul(ps[g][:, 0, tl(t)], ones[:, :], w_bc[g][:, tl(t)], start=True, stop=True)
                    last.then_inc(s["db_ps"], 1)
                for g in range(G):
                    pe.wait_ge(s["m_lo"], n[g])
                    pe.wait_ge(s["HTs"], n[g])
                    for d in range(DT):
                        last = incidence_product(bank(g, 1)[:, d], lambda k, b: RA[g][:, b, k, tl(d)],
                                                 lambda k, b: HT[g][:, k, :], NT)
                    last.then_inc(s["uT_ps"], 1)
                for g in range(G):
                    pe.wait_ge(s["u_lo"], n[g])
                    w1 = (w1_hi, w1_lo)
                    for h in range(HT_):
                        last = product(bank(g, h // 2)[:, h % 2], lambda k, a: w1[a][:, k, tl(h)],
                                       lambda k, b: RB[g][:, b, k], DT)
                    last.then_inc(s["h_ps"], 1)
                for g in range(G):
                    pe.wait_ge(s["r"], n[g])
                    for t in range(NT):
                        last = plain(ps[g][:, t, 0:D + 1], lambda k: R4[g][:, k, tl(t)], lambda k: w2c[:, k, :], HT_)
                    last.then_inc(s["y_ps"], 1)
                for g in range(G):
                    pe.wait_ge(s["sqs"], n[g])
                    for t in range(NT):
                        last = pe.matmul(ps[g][:, t, D + 1:D + 2], F[g][:, 2, tl(t)], ones[:, 0:1],
                                         start=True, stop=True)
                    last.then_inc(s["ss_ps"], 1)
                for g in range(G):
                    pe.wait_ge(s["yf_lo"], n[g])
                    for t in range(NT):
                        last = incidence_product(bank(g, 0)[:, t], lambda k, b: H[g][:, k, tl(t)],
                                                 lambda k, b: RA[g][:, b, k], NT)
                    last.then_inc(s["m2_ps"], 1)
                for g in range(G):
                    pe.wait_ge(s["m2_lo"], n[g])
                    for t in range(NT):
                        last = incidence_product(bank(g, 1)[:, t], lambda k, b: HT[g][:, k, tl(t)],
                                                 lambda k, b: RB[g][:, b, k], NT)
                    last.then_inc(s["u2_ps"], 1)
                for g in range(G):
                    pe.wait_ge(s["x3"], n[g])
                    transpose(X[g], g).then_inc(s["x3T_ps"], 1)
                for g in range(G):
                    pe.wait_ge(s["x3T_lo"], n[g])
                    w3 = (w3_hi, w3_lo)
                    for b, half, done in ((1, 1, "yb_ps"), (0, 0, "ya_ps")):
                        for t in range(NT):
                            last = product(bank(g, b)[:, t], lambda k, a: RA[g][:, a, k, tl(t)],
                                           lambda k, c: w3[c][:, half * DT + k, :], DT)
                        last.then_inc(s[done], 1)
                for g in range(G):
                    pe.wait_ge(s["yb"], n[g])
                    pe.wait_ge(s["ya"], n[g])
                    for t in range(NT):
                        last = plain(ps[g][:, t, 0:D + 1], lambda k: adjT[g][:, k, tl(t)], lambda k: Y[g][:, k, :], NT)
                    last.then_inc(s["ag_ps"], 1)


def kernel(**inputs):
    import numpy as np
    import concourse.bacc as bacc
    from concourse.bass_utils import run_bass_kernel_spmd

    a = {k: np.asarray(v) for k, v in inputs.items()}
    arrays = {
        "x": a["x"], "xT": a["x"].transpose(0, 2, 1), "adj": a["adj"], "adjT": a["adj"].transpose(0, 2, 1),
        "Wq": a["L0_gnn_Wq_w"], "bq": a["L0_gnn_Wq_b"], "Wkey": a["L0_gnn_Wk_w"], "bkey": a["L0_gnn_Wk_b"],
        "WvT": a["L0_gnn_Wv_w"].T, "bv": a["L0_gnn_Wv_b"],
        "aVT": a["L1_gnn_Wv"].T, "abv": a["L1_gnn_bv"], "aw": a["L1_gnn_aw"].reshape(-1), "ab": a["L1_gnn_ab"],
        "Wk": a["L1_gnn_Wk"], "bk": a["L1_gnn_bk"],
        "W1T": a["L2_gnn_W1"].T, "b1": a["L2_gnn_b1"], "gamma": a["L2_gnn_gamma"], "beta": a["L2_gnn_beta"],
        "W2T": a["L2_gnn_W2"].T, "b2": a["L2_gnn_b2"],
        "W3T": a["L3_gnn_W"].T,
    }
    nc = bacc.Bacc("TRN2", target_bir_lowering=False, num_devices=1)
    aps, feed = {}, {}
    for name, v in arrays.items():
        feed[f"in_{name}"] = np.ascontiguousarray(v)
        aps[name] = nc.dram_tensor(f"in_{name}", v.shape, F32, kind="ExternalInput").ap()
    aps["out"] = nc.dram_tensor("out_x", a["x"].shape, F32, kind="ExternalOutput").ap()
    build_graph_stack(nc, aps)
    r = run_bass_kernel_spmd(nc, [feed], core_ids=[0])
    return r.results[0]["out_x"]
```

```python
from contextlib import ExitStack

import concourse.bass as bass
from concourse import mybir

F32 = mybir.dt.float32
F32R = mybir.dt.float32r
ALU = mybir.AluOpType
ACT = mybir.ActivationFunctionType

P = 128
LN_EPS = 1e-5
TINY = 1.2e-38
G = 4
LAGS = 4


def walk(eng, B, tick):
    def peeled(k):
        def run(step, lag):
            m = k - lag
            if 0 <= m < B:
                step(m % G, m + 1, m + 1 + G, 16 * (m // G) + 16)
        tick(run)

    for k in range(G):
        peeled(k)
    with eng.Fori(G, B, G) as i:
        count = {o: eng.snap(i + (o + 1)) for o in range(1 - LAGS, 2 * G)}
        loads = {o: eng.snap(i * (16 // G) + (16 + 16 // G * o)) for o in (-G, 0)}
        for q in range(G):
            def run(step, lag):
                o = q - lag
                step(o % G, count[o], count[o + G], loads[o - o % G])
            tick(run)
    for k in range(B, B + LAGS - 1):
        peeled(k)


def build_graph_stack(nc, A):
    B, N, D = A["x"].shape
    DH = A["W1T"].shape[1]
    K = A["Wk"].shape[0]
    NT = N // P
    DT = D // P
    HT_ = DH // P
    DY = D + 2
    assert NT == 2 and DT == 2 and HT_ == 4 and N == D == 256 and B % G == 0 and K == 3 and LAGS == G

    ctx = ExitStack()
    with ctx:
        def sb(name, shape, dt=F32):
            return ctx.enter_context(nc.sbuf_tensor(name, shape, dt))

        def sem(name):
            return ctx.enter_context(nc.semaphore(name))

        def per_slot(name, shape, dt=F32):
            return [sb(f"{name}{g}", shape, dt) for g in range(G)]

        qk_hi, qk_lo = sb("qk_hi", [P, DT, D], F32R), sb("qk_lo", [P, DT, D], F32R)
        v_hi, v_lo = sb("v_hi", [P, DT, D], F32R), sb("v_lo", [P, DT, D], F32R)
        wk_hi, wk_lo = sb("wk_hi", [P, DT, K, D], F32R), sb("wk_lo", [P, DT, K, D], F32R)
        w1_hi, w1_lo = sb("w1_hi", [P, DT, DH], F32R), sb("w1_lo", [P, DT, DH], F32R)
        w3_hi, w3_lo = sb("w3_hi", [P, 2 * DT, D], F32R), sb("w3_lo", [P, 2 * DT, D], F32R)
        si_hi, si_lo = sb("si_hi", [P, DT, P], F32R), sb("si_lo", [P, DT, P], F32R)
        w2_hi, w2_lo = sb("w2_hi", [P, HT_, DY], F32R), sb("w2_lo", [P, HT_, DY], F32R)
        row_rep = sb("row_rep", [P, DT, P], F32R)
        ident = sb("ident", [P, P])
        ones = sb("ones", [P, P])
        bv_bc = sb("bv_bc", [P, D])
        bk_bc = sb("bk_bc", [P, D])
        sj_bc = sb("sj_bc", [P, D])
        w2b_bc = sb("w2b_bc", [P, D])
        b2_bc = sb("b2_bc", [P, D])
        b1_col = sb("b1_col", [P, HT_])
        qk_col = sb("qk_col", [P, DT])
        bqbk = sb("bqbk", [P, 1])
        e_const = sb("e_const", [P, 1])
        cols = sb("cols", [P, 24])
        minus_half = sb("minus_half", [P, 2])
        minus_one = sb("minus_one", [P, 2])
        eps_col = sb("eps_col", [P, 2])

        x = per_slot("x", [P, NT, D])
        xT = per_slot("xT", [P, DT, N])
        adj = per_slot("adj", [P, NT, N])
        adjT = per_slot("adjT", [P, NT, N])
        w_bc = per_slot("w_bc", [P, N])
        RA = per_slot("RA", [P, 2, 2, 256], F32R)
        RB = per_slot("RB", [P, 2, 2, 256], F32R)
        H = per_slot("H", [P, NT, N], F32R)
        HT = per_slot("HT", [P, NT, N], F32R)
        F = per_slot("F", [P, 4, 256])
        Y = per_slot("Y", [P, 2, NT, DY], F32R)
        R4 = per_slot("R4", [P, 4, 256])
        X = per_slot("X", [P, NT, D])
        sm = per_slot("sm", [P, 64])
        ps = [ctx.enter_context(nc.psum_tensor(f"ps{g}", [P, 2, 512], F32)) for g in range(G)]

        def stats(g, t):
            return sm[g][:, 6 * t:6 * t + 6]

        def mv(g):
            return sm[g][:, 12:16].rearrange("p (t c) -> p t c", c=2)

        def rstd(g):
            return sm[g][:, 16:18]

        def rinv(g):
            return sm[g][:, 18:20]

        def rsum(g):
            return sm[g][:, 20:22]

        def sj_col(g):
            return sm[g][:, 22:24]

        def deg(g):
            return sm[g][:, 24:28]

        def deg_mask(g):
            return sm[g][:, 28:32]

        def deg_safe(g):
            return sm[g][:, 32:36]

        def deg_inv(g):
            return sm[g][:, 36:40]

        def hmom(g):
            return sm[g][:, 40:44].rearrange("p (t c) -> p t c", c=2)

        def hmean2(g):
            return sm[g][:, 44:46]

        def hvar(g):
            return sm[g][:, 46:48]

        def veps(g):
            return sm[g][:, 48:50]

        def sjraw(g):
            return sm[g][:, 50:52]

        def neg_mean(g):
            return sm[g][:, 52:54]

        def nbias(g):
            return sm[g][:, 54:56]

        def bank(g, b):
            return ps[g][:, b, :].rearrange("p (t n) -> p t n", t=2)

        def tl(t):
            return slice(t * P, (t + 1) * P)

        def four(buf, part):
            return buf[:, part // 2, part % 2]

        ld_xT = [sem(f"ld_xT{g}") for g in range(G)]
        ld_x = [sem(f"ld_x{g}") for g in range(G)]
        ld_adj = [sem(f"ld_adj{g}") for g in range(G)]
        ld_adjT = [sem(f"ld_adjT{g}") for g in range(G)]
        ld_w = [sem(f"ld_w{g}") for g in range(G)]
        stored = [sem(f"stored{g}") for g in range(G)]
        names = """xT_hi xT_lo xb t_ps t_hi t_lo sT_ps v_ps eT v_hi v_lo pT pT_hi pT_lo pv_ps inv0 z0
            st0 mv0  ve0 rs0 nb0 x1
            x1T_ps x1T_hi x1T_lo sjr sjc y2_ps y2_hi y2_lo si_ps zs lk e1 T T_hi T_lo y1_ps y0_ps y1 y0
            z1_ps den1 inv1 w1 w1_hi w1_lo z2_ps h1 z1n st1 mv1  ve1 rs1 nb1 x2
            H HT dn  dsafe drec dinv diag
            x2_hi x2_lo x2b m_ps db_ps m_hi m_lo dbc uT_ps u u_hi u_lo h_ps r sq r_hi r_lo sqa  sqs y_ps ss_ps
             hst hm2 hv ve2 rs2 yf yf_hi yf_lo m2_ps m2_hi m2_lo u2_ps z3 st3 mv3  ve3 rs3 nb3 x3
            x3T_ps x3T_hi x3T_lo yb_ps yb_hi yb_lo ya_ps ya aT_hi aT_lo ag_ps den4 inv4 agz
            banks_free st4 mv4  ve4 rs4 nb4 outp""".split()
        s = {name: sem(name) for name in names}
        stats_seen = sem("stats_seen")
        ld_w0, ld_w1 = sem("ld_w_first"), sem("ld_w_second")
        p_const = sem("p_const")
        p_rep = sem("p_rep")
        p_mm = sem("p_mm")
        p_ev = sem("p_ev")
        p_done = sem("p_done")

        st_wq, st_wk = R4[0][:, 0:2, :], R4[0][:, 2:4, :]
        st_vT = R4[1][:, 0:2, :]
        st_aVT = R4[1][:, 2:4, :]
        st_kw = [R4[2][:, 0:2, :], R4[2][:, 2:4, :], R4[3][:, 0:2, :]]
        st_w1 = F[0][:, :, :].rearrange("p (k a) n -> p k (a n)", k=DT)
        st_w2 = F[1]
        st_w3 = F[2]
        st_bk3 = F[3][:, 0:3, :]
        gam_w2 = R4[0]
        bq_col, bk_col = cols[:, 0:2], cols[:, 2:4]
        awj_col, awi_col = cols[:, 4:6], cols[:, 6:8]
        abv_col = cols[:, 8:10]
        gam_col, bet_col = cols[:, 10:14], cols[:, 14:18]
        ab_col = cols[:, 18:19]
        aw_sum = cols[:, 20:22]
        rep_bk = X[0][:, :, 0:P]
        rep_awj = X[0][:, :, P:2 * P]
        rep_awi = X[1][:, :, 0:P]
        rep_aws = X[1][:, :, P:2 * P]
        rep_bet = X[2][:, :, :].rearrange("p t (a n) -> p (t a) n", a=2)

        block = ctx.enter_context(nc.Block())

        @block.sync
        def _(sp):
            def tiles(ap):
                return ap.rearrange("(t p) n -> p t n", p=P)

            def column(ap, k):
                return ap.rearrange("(t p) -> p t", p=P)[:, 0:k]

            def first_load(g):
                for dst, name, sems in ((xT, "xT", ld_xT), (x, "x", ld_x), (adjT, "adjT", ld_adjT), (adj, "adj", ld_adj)):
                    sp.dma_start(dst[g][:, :, :], tiles(A[name][g])).then_inc(sems[g], 16)
                sp.dma_start(w_bc[g][:, :], A["adj"][g, 0, :].partition_broadcast(P)).then_inc(ld_w[g], 16)

            for g in range(G):
                sp.sem_inc(stored[g], 16)
            with nc.allow_non_contiguous_dma(reason="weight vectors as columns, once"):
                for dst, src in (
                    (st_wq, tiles(A["Wq"])), (st_wk, tiles(A["Wkey"])),
                    (bq_col, column(A["bq"], DT)), (bk_col, column(A["bkey"], DT)),
                    (st_aVT, tiles(A["aVT"])),
                    (awj_col, column(A["aw"][0:D], DT)), (awi_col, column(A["aw"][D:2 * D], DT)),
                    (abv_col, column(A["abv"], DT)), (ab_col, A["ab"].partition_broadcast(P)),
                    (gam_col, column(A["gamma"], HT_)), (bet_col, column(A["beta"], HT_)),
                ):
                    sp.dma_start(dst, src).then_inc(ld_w0, 16)
                sp.dma_start(b1_col[:, :], column(A["b1"], HT_)).then_inc(ld_w1, 16)
            for dst, src in (
                (st_vT, tiles(A["WvT"])), (st_w2[:, :, :], tiles(A["W2T"])),
                (bv_bc[:, :], A["bv"].partition_broadcast(P)),
                (st_kw[0], tiles(A["Wk"][0])), (st_kw[1], tiles(A["Wk"][1])), (st_kw[2], tiles(A["Wk"][2])),
                (st_bk3, A["bk"].partition_broadcast(P)), (b2_bc[:, :], A["b2"].partition_broadcast(P)),
            ):
                sp.dma_start(dst, src).then_inc(ld_w1, 16)
            sp.dma_start(st_w1, tiles(A["W1T"])).then_inc(ld_w1, 16)
            sp.dma_start(st_w3[:, :, :], tiles(A["W3T"])).then_inc(ld_w1, 16)
            for g in range(G):
                first_load(g)

            def slot(name, g):
                return A[name].rearrange("(j g) r n -> g j r n", g=G)[g]

            def graph(name, j, g):
                return slot(name, g)[bass.ds(j, 1), :, :].rearrange("a (t p) n -> p (a t) n", p=P)

            with sp.Fori(0, B // G - 1, 1) as j:
                for g in range(G):
                    n = sp.snap(j * G + (g + 1))
                    sp.wait_ge(s["xT_lo"], n)
                    sp.dma_start(xT[g][:, :, :], graph("xT", j + 1, g)).then_inc(ld_xT[g], 16)
                    sp.wait_ge(s["z0"], n)
                    sp.dma_start(x[g][:, :, :], graph("x", j + 1, g)).then_inc(ld_x[g], 16)
                    sp.wait_ge(s["db_ps"], n)
                    sp.dma_start(w_bc[g][:, :],
                                 slot("adj", g)[bass.ds(j + 1, 1), 0, :].rearrange("a n -> (a n)").partition_broadcast(P))\
                        .then_inc(ld_w[g], 16)
                    sp.wait_ge(s["u"], n)
                    sp.dma_start(adj[g][:, :, :], graph("adj", j + 1, g)).then_inc(ld_adj[g], 16)
                    sp.wait_ge(s["aT_lo"], n)
                    sp.dma_start(adjT[g][:, :, :], graph("adjT", j + 1, g)).then_inc(ld_adjT[g], 16)
                    sp.wait_ge(s["outp"], n)
                    sp.dma_start(graph("out", j, g), R4[g][:, 2:4, :]).then_inc(stored[g], 16)
            for g in range(G):
                sp.wait_ge(s["outp"], B - G + g + 1)
                sp.dma_start(tiles(A["out"][B - G + g]), R4[g][:, 2:4, :]).then_inc(stored[g], 16)
            for g in range(G):
                sp.wait_ge(stored[g], 16 * (B // G + 1))

        @block.gpsimd
        def _(pool):
            pool.memset(ones[:, :], 1.0)
            pool.memset(eps_col[:, :], LN_EPS)
            pool.memset(minus_one[:, :], -1.0)
            pool.memset(minus_half[:, :], -0.5).then_inc(p_const, 1)
            pool.memset(ident[:, :], 0.0).then_inc(p_const, 1)
            pool.wait_ge(p_const, 2)
            pool.affine_select(out=ident[:, :], in_=ident[:, :], compare_op=ALU.not_equal, fill=1.0,
                               base=0, pattern=[[-1, P]], channel_multiplier=1).then_inc(p_const, 1)
            pool.wait_ge(p_const, 3)
            pool.wait_ge(p_done, 1)

            def low_part(lo, full, hi, done):
                pool.tensor_tensor(lo, full, hi.bitcast(F32), ALU.subtract).then_inc(s[done], 1)

            def rsqrt(var, l, n, g):
                pool.tensor_tensor(veps(g), var, eps_col[:, :], ALU.add).then_inc(s["ve" + l], 1)
                pool.wait_ge(s["ve" + l], n)
                pool.tensor_tensor(rstd(g), veps(g), minus_half[:, :], ALU.pow).then_inc(s["rs" + l], 1)

            def norm_scalars(l, n, g):
                pool.wait_ge(s["mv" + l], n)
                pool.tensor_tensor(neg_mean(g), mv(g)[:, :, 0], minus_one[:, :], ALU.mult)
                rsqrt(mv(g)[:, :, 1], l, n, g)
                pool.wait_ge(s["rs" + l], n)
                pool.tensor_tensor(nbias(g), neg_mean(g), rstd(g), ALU.mult).then_inc(s["nb" + l], 1)

            def xT_lo(g, n, nn, l16):
                pool.wait_ge(s["xT_hi"], n)
                low_part(RA[g][:, 1], xT[g][:, :, :], RA[g][:, 0], "xT_lo")

            def xb(g, n, nn, l16):
                pool.wait_ge(ld_x[g], l16)
                pool.tensor_tensor(x[g][:, :, :], x[g][:, :, :],
                                   bv_bc[:, None, :].to_broadcast([P, NT, D]), ALU.add).then_inc(s["xb"], 1)

            def pT(g, n, nn, l16):
                pool.wait_ge(s["eT"], n)
                pool.wait_ge(ld_adjT[g], l16)
                pool.tensor_tensor(F[g][:, 0:2, :], F[g][:, 0:2, :], adjT[g][:, :, :], ALU.mult)\
                    .then_inc(s["pT"], 1)

            def pT_lo(g, n, nn, l16):
                pool.wait_ge(s["pT_hi"], n)
                low_part(RB[g][:, 1], F[g][:, 0:2, :], RB[g][:, 0], "pT_lo")

            def rs0(g, n, nn, l16):
                norm_scalars("0", n, g)

            def diag(g, n, nn, l16):
                pool.wait_ge(s["dinv"], n)
                for t in range(NT):
                    last = pool.tensor_tensor(w_bc[g][:, tl(t)], ident[:, :],
                                              deg_inv(g)[:, t:t + 1].to_broadcast([P, P]), ALU.mult)
                last.then_inc(s["diag"], 1)

            def T(g, n, nn, l16):
                pool.wait_ge(s["e1"], n)
                pool.tensor_tensor(F[g][:, 0:2, :], F[g][:, 0:2, :], adjT[g][:, :, :], ALU.mult)\
                    .then_inc(s["T"], 1)

            def T_lo(g, n, nn, l16):
                pool.wait_ge(s["T_hi"], n)
                low_part(RB[g][:, 1], F[g][:, 0:2, :], RB[g][:, 0], "T_lo")

            def w1_lo(g, n, nn, l16):
                pool.wait_ge(s["w1_hi"], n)
                low_part(RA[g][:, 1], R4[g][:, 0:2, :], RA[g][:, 0], "w1_lo")

            def rs1(g, n, nn, l16):
                norm_scalars("1", n, g)

            def x2_lo(g, n, nn, l16):
                pool.wait_ge(s["x2_hi"], n)
                low_part(RB[g][:, 1], X[g][:, :, :], RB[g][:, 0], "x2_lo")

            def u_lo(g, n, nn, l16):
                pool.wait_ge(s["u_hi"], n)
                low_part(RB[g][:, 1], F[g][:, 0:2, :], RB[g][:, 0], "u_lo")

            def r_lo(g, n, nn, l16):
                pool.wait_ge(s["r_hi"], n)
                low_part(RB[g][:, :, :, :].rearrange("p a b n -> p (a b) n"), R4[g][:, :, :],
                         RA[g][:, :, :, :].rearrange("p a b n -> p (a b) n"), "r_lo")

            def rs2(g, n, nn, l16):
                pool.wait_ge(s["hv"], n)
                rsqrt(hvar(g), "2", n, g)

            def yf_lo(g, n, nn, l16):
                pool.wait_ge(s["yf_hi"], n)
                low_part(RA[g][:, 1], F[g][:, 2:4, :], RA[g][:, 0], "yf_lo")

            def rs3(g, n, nn, l16):
                norm_scalars("3", n, g)

            def aT_lo(g, n, nn, l16):
                pool.wait_ge(s["aT_hi"], n)
                low_part(RB[g][:, 1], adjT[g][:, :, :], RB[g][:, 0], "aT_lo")

            def rs4(g, n, nn, l16):
                norm_scalars("4", n, g)

            def tick(run):
                run(T_lo, 1)
                run(xT_lo, 0)
                run(u_lo, 2)
                run(rs3, 3)
                run(w1_lo, 1)
                run(aT_lo, 3)
                run(xb, 0)
                run(pT, 0)
                run(diag, 1)
                run(pT_lo, 0)
                run(r_lo, 2)
                run(rs1, 1)
                run(rs0, 0)
                run(x2_lo, 1)
                run(rs4, 3)
                run(rs2, 2)
                run(yf_lo, 2)
                run(T, 0)

            walk(pool, B, tick)

        @block.scalar
        def _(act):
            act.wait_ge(p_done, 1)

            def high_part(hi, full, done):
                act.activation(hi, full, ACT.Copy).then_inc(s[done], 1)

            def normalise(dst, src, l, done, n, g):
                act.wait_ge(s["nb" + l], n)
                for t in range(NT):
                    last = act.activation(dst[:, t, :], src[:, t, :], ACT.Identity,
                                          bias=nbias(g)[:, t:t + 1], scale=rstd(g)[:, t:t + 1])
                last.then_inc(s[done], 1)

            def xT_hi(g, n, nn, l16):
                act.wait_ge(ld_xT[g], l16)
                high_part(RA[g][:, 0], xT[g][:, :, :], "xT_hi")

            def t_hi(g, n, nn, l16):
                act.wait_ge(s["t_ps"], n)
                for d in range(DT):
                    last = act.activation(RB[g][:, 0, d], bank(g, 0)[:, d], ACT.Identity, bias=qk_col[:, d:d + 1])
                last.then_inc(s["t_hi"], 1)

            def eT(g, n, nn, l16):
                act.wait_ge(s["sT_ps"], n)
                act.activation(F[g][:, 0:2, :], bank(g, 1), ACT.Exp, bias=bqbk[:, 0:1]).then_inc(s["eT"], 1)

            def v_hi_step(g, n, nn, l16):
                act.wait_ge(s["v_ps"], n)
                high_part(Y[g][:, 0, :, 0:D], bank(g, 0), "v_hi")

            def pT_hi(g, n, nn, l16):
                act.wait_ge(s["pT"], n)
                high_part(RB[g][:, 0], F[g][:, 0:2, :], "pT_hi")

            def x1(g, n, nn, l16):
                normalise(X[g], F[g][:, 2:4, :], "0", "x1", n, g)

            def x1T_hi(g, n, nn, l16):
                act.wait_ge(s["x1T_ps"], n)
                high_part(RA[g][:, 0], bank(g, 0), "x1T_hi")

            def y2_hi(g, n, nn, l16):
                act.wait_ge(s["y2_ps"], n)
                high_part(Y[g][:, 0, :, 0:D], bank(g, 1), "y2_hi")

            def zs(g, n, nn, l16):
                act.wait_ge(s["si_ps"], n)
                act.wait_ge(s["sjc"], n)
                for t in range(NT):
                    last = act.activation(F[g][:, t, :], bank(g, 0)[:, 0], ACT.Identity, bias=sj_col(g)[:, t:t + 1])
                last.then_inc(s["zs"], 1)

            def e1(g, n, nn, l16):
                act.wait_ge(s["lk"], n)
                act.activation(F[g][:, 0:2, :], F[g][:, 2:4, :], ACT.Exp).then_inc(s["e1"], 1)

            def T_hi(g, n, nn, l16):
                act.wait_ge(s["T"], n)
                high_part(RB[g][:, 0], F[g][:, 0:2, :], "T_hi")

            def y1_sb(g, n, nn, l16):
                act.wait_ge(s["y1_ps"], n)
                act.activation(R4[g][:, 0:2, :], bank(g, 1), ACT.Copy).then_inc(s["y1"], 1)

            def w1_hi_step(g, n, nn, l16):
                act.wait_ge(s["w1"], n)
                high_part(RA[g][:, 0], R4[g][:, 0:2, :], "w1_hi")

            def x2(g, n, nn, l16):
                normalise(X[g], F[g][:, 0:2, :], "1", "x2", n, g)

            def x2_hi(g, n, nn, l16):
                act.wait_ge(s["x2"], n)
                high_part(RB[g][:, 0], X[g][:, :, :], "x2_hi")

            def m_hi(g, n, nn, l16):
                act.wait_ge(s["m_ps"], n)
                for t in range(NT):
                    last = act.activation(RA[g][:, 0, t], bank(g, 1)[:, t], ACT.Copy, scale=deg_inv(g)[:, 2 + t:3 + t])
                last.then_inc(s["m_hi"], 1)

            def dbc(g, n, nn, l16):
                act.wait_ge(s["db_ps"], n)
                act.activation(adj[g][:, 0, :], bank(g, 0)[:, 0], ACT.Copy).then_inc(s["dbc"], 1)

            def u_hi(g, n, nn, l16):
                act.wait_ge(s["u"], n)
                high_part(RB[g][:, 0], F[g][:, 0:2, :], "u_hi")

            def r(g, n, nn, l16):
                act.wait_ge(s["h_ps"], n)
                for k in range(HT_):
                    last = act.activation(R4[g][:, k, :], bank(g, k // 2)[:, k % 2], ACT.Relu, bias=b1_col[:, k:k + 1])
                last.then_inc(s["r"], 1)

            def sq(g, n, nn, l16):
                act.wait_ge(s["r"], n)
                act.wait_ge(s["u_lo"], n)
                act.activation(F[g][:, :, :], R4[g][:, :, :], ACT.Square).then_inc(s["sq"], 1)

            def r_hi(g, n, nn, l16):
                act.wait_ge(s["r"], n)
                high_part(RA[g][:, :, :, :].rearrange("p a b n -> p (a b) n"), R4[g][:, :, :], "r_hi")

            def yf_hi(g, n, nn, l16):
                act.wait_ge(s["yf"], n)
                high_part(RA[g][:, 0], F[g][:, 2:4, :], "yf_hi")

            def m2_hi(g, n, nn, l16):
                act.wait_ge(s["m2_ps"], n)
                for t in range(NT):
                    last = act.activation(RB[g][:, 0, t], bank(g, 0)[:, t], ACT.Copy, scale=deg_inv(g)[:, 2 + t:3 + t])
                last.then_inc(s["m2_hi"], 1)

            def x3(g, n, nn, l16):
                normalise(X[g], F[g][:, 0:2, :], "3", "x3", n, g)

            def x3T_hi(g, n, nn, l16):
                act.wait_ge(s["x3T_ps"], n)
                high_part(RA[g][:, 0], bank(g, 0), "x3T_hi")

            def yb_hi(g, n, nn, l16):
                act.wait_ge(s["yb_ps"], n)
                high_part(Y[g][:, 0, :, 0:D], bank(g, 1), "yb_hi")

            def ya_sb(g, n, nn, l16):
                act.wait_ge(s["ya_ps"], n)
                act.activation(R4[g][:, 0:2, :], bank(g, 0), ACT.Copy).then_inc(s["ya"], 1)

            def aT_hi(g, n, nn, l16):
                act.wait_ge(s["u2_ps"], n)
                high_part(RB[g][:, 0], adjT[g][:, :, :], "aT_hi")

            def outp(g, n, nn, l16):
                normalise(R4[g][:, 2:4, :], F[g][:, 2:4, :], "4", "outp", n, g)

            def tick(run):
                run(dbc, 2)
                run(m2_hi, 3)
                run(T_hi, 1)
                run(xT_hi, 0)
                run(y1_sb, 1)
                run(u_hi, 2)
                run(aT_hi, 3)
                run(t_hi, 0)
                run(w1_hi_step, 1)
                run(x3, 3)
                run(r, 2)
                run(eT, 0)
                run(x3T_hi, 3)
                run(sq, 2)
                run(pT_hi, 0)
                run(v_hi_step, 0)
                run(r_hi, 2)
                run(yb_hi, 3)
                run(ya_sb, 3)
                run(x2, 1)
                run(x2_hi, 1)
                run(x1, 0)
                run(x1T_hi, 0)
                run(outp, 3)
                run(zs, 0)
                run(yf_hi, 2)
                run(m_hi, 1)
                run(e1, 0)
                run(y2_hi, 0)

            walk(act, B, tick)

        @block.vector
        def _(dve):
            ev = [0]

            def step(ins):
                ins.then_inc(p_ev, 1)
                ev[0] += 1
                dve.wait_ge(p_ev, ev[0])

            dve.sem_inc(s["banks_free"], G)
            for lo_zero in [Y[g][:, 1, :, D:DY] for g in range(G)] + [w2_lo[:, :, D:DY]]:
                dve.memset(lo_zero.bitcast(F32), 0.0)
            for hi_one in [Y[g][:, 0, :, D:D + 1] for g in range(G)] + [w2_hi[:, :, D:D + 1]]:
                dve.memset(hi_one.bitcast(F32), 1.0)
            for hi_zero in [Y[g][:, 0, :, D + 1:DY] for g in range(G)] + [w2_hi[:, :, D + 1:DY]]:
                dve.memset(hi_zero.bitcast(F32), 0.0)
            dve.wait_ge(ld_w0, 16 * 11)
            dve.wait_ge(p_const, 1)
            step(dve.tensor_tensor(aw_sum, awj_col, awi_col, ALU.add))
            for k in range(HT_):
                dve.tensor_scalar(rep_bet[:, k, :], ones[:, :], bet_col[:, k:k + 1], None, ALU.mult)
            for t in range(2):
                for rep, col in ((rep_bk, bk_col), (rep_awj, awj_col), (rep_awi, awi_col), (rep_aws, aw_sum)):
                    last = dve.tensor_scalar(rep[:, t, :], ones[:, :], col[:, t:t + 1], None, ALU.mult)
            last.then_inc(p_rep, 1)
            dve.wait_ge(ld_w1, 16 * 11)
            dve.wait_ge(p_mm, 1)
            for k in range(HT_):
                last = dve.tensor_scalar(gam_w2[:, k, :], st_w2[:, k, :], gam_col[:, k:k + 1], None, ALU.mult)
            last.then_inc(p_rep, 1)
            dve.tensor_copy(qk_hi[:, :, :], bank(0, 0))
            dve.tensor_copy(si_hi[:, :, :], bank(1, 0)[:, :, 0:P])
            dve.tensor_copy(row_rep[:, :, :], bank(1, 1)[:, :, 0:P])
            dve.tensor_copy(sj_bc[:, :], bank(2, 0)[:, 0])
            dve.tensor_copy(w2b_bc[:, :], bank(2, 1)[:, 0])
            dve.tensor_copy(qk_col[:, :], ps[3][:, 0, 0:2])
            dve.tensor_copy(bqbk[:, :], ps[3][:, 0, 2:3])
            step(dve.tensor_tensor(e_const[:, :], ps[3][:, 0, 3:4], ab_col, ALU.add))
            dve.tensor_tensor(qk_lo[:, :, :], bank(0, 0), qk_hi[:, :, :].bitcast(F32), ALU.subtract)
            dve.tensor_tensor(si_lo[:, :, :], bank(1, 0)[:, :, 0:P], si_hi[:, :, :].bitcast(F32), ALU.subtract)
            pairs = [(v_hi[:, :, :], v_lo[:, :, :], st_vT)]
            pairs += [(wk_hi[:, :, k, :], wk_lo[:, :, k, :], st_kw[k]) for k in range(K)]
            pairs += [(w1_hi[:, :, :], w1_lo[:, :, :], st_w1), (w3_hi[:, :, :], w3_lo[:, :, :], st_w3[:, :, :])]
            for hi, lo, full in pairs:
                last = dve.tensor_copy(hi, full)
            step(last)
            for hi, lo, full in pairs:
                dve.tensor_tensor(lo, full, hi.bitcast(F32), ALU.subtract)
            step(dve.tensor_tensor(bk_bc[:, :], st_bk3[:, 0, :], st_bk3[:, 1, :], ALU.add))
            step(dve.tensor_tensor(bk_bc[:, :], bk_bc[:, :], st_bk3[:, 2, :], ALU.add))
            dve.wait_ge(p_mm, 2)
            for k in range(HT_):
                last = dve.scalar_tensor_tensor(st_w2[:, k, :], ps[3][:, 1, 0:D], -1.0 / DH, gam_w2[:, k, :],
                                                ALU.mult, ALU.add)
            step(last)
            step(dve.tensor_copy(w2_hi[:, :, 0:D], st_w2[:, :, :]))
            dve.tensor_tensor(w2_lo[:, :, 0:D], st_w2[:, :, :], w2_hi[:, :, 0:D].bitcast(F32), ALU.subtract)\
                .then_inc(p_done, 1)
            dve.wait_ge(p_done, 1)

            def layer_norm_stats(src, l, n, g):
                for t in range(NT):
                    last = dve.bn_stats(stats(g, t), src[:, t, :])
                last.then_inc(s["st" + l], 1)
                dve.wait_ge(s["st" + l], n)
                dve.sem_inc(stats_seen, 1)
                for t in range(NT):
                    last = dve.bn_aggr(mv(g)[:, t, :], stats(g, t))
                last.then_inc(s["mv" + l], 1)

            def low_part(lo, full, hi, done):
                dve.tensor_tensor(lo, full, hi.bitcast(F32), ALU.subtract).then_inc(s[done], 1)

            def t_lo(g, n, nn, l16):
                dve.wait_ge(s["t_hi"], n)
                for d in range(DT):
                    last = dve.scalar_tensor_tensor(RB[g][:, 1, d], bank(g, 0)[:, d], qk_col[:, d:d + 1],
                                                    RB[g][:, 0, d].bitcast(F32), ALU.add, ALU.subtract)
                last.then_inc(s["t_lo"], 1)

            def v_lo_step(g, n, nn, l16):
                dve.wait_ge(s["v_hi"], n)
                low_part(Y[g][:, 1, :, 0:D], bank(g, 0), Y[g][:, 0, :, 0:D], "v_lo")

            def H_step(g, n, nn, l16):
                dve.wait_ge(ld_adj[g], l16)
                dve.tensor_scalar(H[g][:, :, :], adj[g][:, :, :], 0.0, None, ALU.not_equal).then_inc(s["H"], 1)

            def HT_step(g, n, nn, l16):
                dve.wait_ge(ld_adjT[g], l16)
                for t in range(NT):
                    last = dve.tensor_scalar(HT[g][:, t, :], adjT[g][:, t, :], 0.0, None, ALU.not_equal,
                                             ALU.add, accum_out=deg(g)[:, 2 + t:3 + t])
                last.then_inc(s["HT"], 1)

            def dn(g, n, nn, l16):
                dve.wait_ge(ld_w[g], l16)
                dve.wait_ge(s["H"], n)
                for t in range(NT):
                    last = dve.scalar_tensor_tensor(adj[g][:, t, :], H[g][:, t, :].bitcast(F32), 1.0,
                                                    w_bc[g][:, :], ALU.mult, ALU.mult,
                                                    accum_out=deg(g)[:, t:t + 1])
                last.then_inc(s["dn"], 1)

            def dinv(g, n, nn, l16):
                dve.wait_ge(s["HT"], n)
                dve.wait_ge(s["dn"], n)
                dve.tensor_scalar(deg_mask(g), deg(g), 0.0, None, ALU.is_gt)
                dve.tensor_scalar(deg_safe(g), deg(g), TINY, None, ALU.max).then_inc(s["dsafe"], 1)
                dve.wait_ge(s["dsafe"], n)
                dve.reciprocal(deg_safe(g), deg_safe(g)).then_inc(s["drec"], 1)
                dve.wait_ge(s["drec"], n)
                dve.tensor_tensor(deg_inv(g), deg_safe(g), deg_mask(g), ALU.mult).then_inc(s["dinv"], 1)

            def z0(g, n, nn, l16):
                dve.wait_ge(s["pv_ps"], n)
                dve.reciprocal(rinv(g), ps[g][:, :, D]).then_inc(s["inv0"], 1)
                dve.wait_ge(s["inv0"], n)
                dve.wait_ge(s["xb"], n)
                for t in range(NT):
                    last = dve.scalar_tensor_tensor(F[g][:, 2 + t, :], ps[g][:, t, 0:D], rinv(g)[:, t:t + 1],
                                                    x[g][:, t, :], ALU.mult, ALU.add)
                last.then_inc(s["z0"], 1)

            def stats0(g, n, nn, l16):
                dve.wait_ge(s["z0"], n)
                layer_norm_stats(F[g][:, 2:4, :], "0", n, g)

            def sj(g, n, nn, l16):
                dve.wait_ge(s["x1"], n)
                for t in range(NT):
                    last = dve.scalar_tensor_tensor(F[g][:, 2 + t, :], X[g][:, t, :], 1.0, sj_bc[:, :],
                                                    ALU.mult, ALU.mult, accum_out=sjraw(g)[:, t:t + 1])
                last.then_inc(s["sjr"], 1)
                dve.wait_ge(s["sjr"], n)
                dve.tensor_scalar(sj_col(g), sjraw(g), e_const[:, 0:1], None, ALU.add).then_inc(s["sjc"], 1)

            def x1T_lo(g, n, nn, l16):
                dve.wait_ge(s["x1T_hi"], n)
                low_part(RA[g][:, 1], bank(g, 0), RA[g][:, 0], "x1T_lo")

            def y2_lo(g, n, nn, l16):
                dve.wait_ge(s["y2_hi"], n)
                low_part(Y[g][:, 1, :, 0:D], bank(g, 1), Y[g][:, 0, :, 0:D], "y2_lo")

            def lk(g, n, nn, l16):
                dve.wait_ge(s["zs"], n)
                dve.scalar_tensor_tensor(F[g][:, 2:4, :], F[g][:, 0:2, :], 0.2, F[g][:, 0:2, :],
                                         ALU.mult, ALU.max).then_inc(s["lk"], 1)

            def y0_sb(g, n, nn, l16):
                dve.wait_ge(s["y0_ps"], n)
                dve.wait_ge(stored[g], l16)
                dve.tensor_tensor(R4[g][:, 2:4, :], bank(g, 0),
                                  bk_bc[:, None, :].to_broadcast([P, NT, D]), ALU.add).then_inc(s["y0"], 1)

            def w1(g, n, nn, l16):
                dve.wait_ge(s["z1_ps"], n)
                dve.tensor_scalar(rsum(g), ps[g][:, :, D], 1e-12, None, ALU.add).then_inc(s["den1"], 1)
                dve.wait_ge(s["den1"], n)
                dve.reciprocal(rinv(g), rsum(g)).then_inc(s["inv1"], 1)
                dve.wait_ge(s["inv1"], n)
                for t in range(NT):
                    last = dve.scalar_tensor_tensor(R4[g][:, t, :], ps[g][:, t, 0:D], rinv(g)[:, t:t + 1],
                                                    R4[g][:, t, :], ALU.mult, ALU.add)
                last.then_inc(s["w1"], 1)

            def h1(g, n, nn, l16):
                dve.wait_ge(s["z2_ps"], n)
                for t in range(NT):
                    last = dve.scalar_tensor_tensor(F[g][:, 2 + t, :], bank(g, 0)[:, t], rinv(g)[:, t:t + 1],
                                                    R4[g][:, 2 + t, :], ALU.mult, ALU.add)
                last.then_inc(s["h1"], 1)
                dve.wait_ge(s["h1"], n)
                dve.scalar_tensor_tensor(F[g][:, 0:2, :], F[g][:, 2:4, :], 0.0, X[g][:, :, :],
                                         ALU.max, ALU.add).then_inc(s["z1n"], 1)

            def stats1(g, n, nn, l16):
                dve.wait_ge(s["z1n"], n)
                layer_norm_stats(F[g][:, 0:2, :], "1", n, g)

            def m_lo(g, n, nn, l16):
                dve.wait_ge(s["m_hi"], n)
                for t in range(NT):
                    last = dve.scalar_tensor_tensor(RA[g][:, 1, t], bank(g, 1)[:, t], deg_inv(g)[:, 2 + t:3 + t],
                                                    RA[g][:, 0, t].bitcast(F32), ALU.mult, ALU.subtract)
                last.then_inc(s["m_lo"], 1)

            def x2b(g, n, nn, l16):
                dve.wait_ge(s["x2_lo"], n)
                dve.scalar_tensor_tensor(X[g][:, :, :], X[g][:, :, :], 2.0,
                                         b2_bc[:, None, :].to_broadcast([P, NT, D]), ALU.mult, ALU.add)\
                    .then_inc(s["x2b"], 1)

            def u(g, n, nn, l16):
                dve.wait_ge(s["uT_ps"], n)
                dve.wait_ge(s["dbc"], n)
                dve.tensor_tensor(F[g][:, 0:2, :], bank(g, 1), adj[g][:, 0:1, :].to_broadcast([P, 2, D]),
                                  ALU.mult).then_inc(s["u"], 1)

            def sqs(g, n, nn, l16):
                dve.wait_ge(s["sq"], n)
                dve.tensor_tensor(F[g][:, 0:2, :], F[g][:, 0:2, :], F[g][:, 2:4, :], ALU.add).then_inc(s["sqa"], 1)
                dve.wait_ge(s["sqa"], n)
                dve.tensor_tensor(F[g][:, 2, :], F[g][:, 0, :], F[g][:, 1, :], ALU.add).then_inc(s["sqs"], 1)

            def hstat(g, n, nn, l16):
                dve.wait_ge(s["ss_ps"], n)
                dve.tensor_scalar(hmom(g), ps[g][:, :, D:DY], 1.0 / DH, None, ALU.mult).then_inc(s["hst"], 1)
                dve.wait_ge(s["hst"], n)
                dve.tensor_tensor(hmean2(g), hmom(g)[:, :, 0], hmom(g)[:, :, 0], ALU.mult).then_inc(s["hm2"], 1)
                dve.wait_ge(s["hm2"], n)
                dve.tensor_tensor(hvar(g), hmom(g)[:, :, 1], hmean2(g), ALU.subtract).then_inc(s["hv"], 1)

            def yf(g, n, nn, l16):
                dve.wait_ge(s["rs2"], n)
                for t in range(NT):
                    last = dve.scalar_tensor_tensor(F[g][:, 2 + t, :], ps[g][:, t, 0:D], rstd(g)[:, t:t + 1],
                                                    w2b_bc[:, :], ALU.mult, ALU.add)
                last.then_inc(s["yf"], 1)

            def m2_lo(g, n, nn, l16):
                dve.wait_ge(s["m2_hi"], n)
                for t in range(NT):
                    last = dve.scalar_tensor_tensor(RB[g][:, 1, t], bank(g, 0)[:, t], deg_inv(g)[:, 2 + t:3 + t],
                                                    RB[g][:, 0, t].bitcast(F32), ALU.mult, ALU.subtract)
                last.then_inc(s["m2_lo"], 1)

            def z3(g, n, nn, l16):
                dve.wait_ge(s["u2_ps"], n)
                dve.wait_ge(s["x2b"], n)
                for t in range(NT):
                    last = dve.scalar_tensor_tensor(F[g][:, t, :], bank(g, 1)[:, t], deg_inv(g)[:, t:t + 1],
                                                    X[g][:, t, :], ALU.mult, ALU.add)
                last.then_inc(s["z3"], 1)

            def stats3(g, n, nn, l16):
                dve.wait_ge(s["z3"], n)
                layer_norm_stats(F[g][:, 0:2, :], "3", n, g)

            def x3T_lo(g, n, nn, l16):
                dve.wait_ge(s["x3T_hi"], n)
                low_part(RA[g][:, 1], bank(g, 0), RA[g][:, 0], "x3T_lo")

            def yb_lo(g, n, nn, l16):
                dve.wait_ge(s["yb_hi"], n)
                low_part(Y[g][:, 1, :, 0:D], bank(g, 1), Y[g][:, 0, :, 0:D], "yb_lo")

            def z4(g, n, nn, l16):
                dve.wait_ge(s["ag_ps"], n)
                dve.tensor_scalar(rsum(g), ps[g][:, :, D], 1e-6, None, ALU.max).then_inc(s["den4"], 1)
                dve.wait_ge(s["den4"], n)
                dve.reciprocal(rinv(g), rsum(g)).then_inc(s["inv4"], 1)
                dve.wait_ge(s["inv4"], n)
                for t in range(NT):
                    last = dve.scalar_tensor_tensor(F[g][:, t, :], ps[g][:, t, 0:D], rinv(g)[:, t:t + 1],
                                                    R4[g][:, t, :], ALU.mult, ALU.add)
                last.then_inc(s["agz"], 1)
                dve.wait_ge(s["agz"], n)
                dve.scalar_tensor_tensor(F[g][:, 2:4, :], F[g][:, 0:2, :], 0.0, X[g][:, :, :],
                                         ALU.max, ALU.add).then_inc(s["banks_free"], 1)

            def stats4(g, n, nn, l16):
                dve.wait_ge(s["banks_free"], nn)
                layer_norm_stats(F[g][:, 2:4, :], "4", n, g)

            def tick(run):
                run(m_lo, 2)
                run(y2_lo, 1)
                run(y0_sb, 1)
                run(m2_lo, 3)
                run(u, 2)
                run(z3, 3)
                run(stats3, 3)
                run(w1, 1)
                run(t_lo, 0)
                run(dn, 1)
                run(dinv, 1)
                run(HT_step, 0)
                run(x2b, 2)
                run(x3T_lo, 3)
                run(h1, 1)
                run(sqs, 2)
                run(v_lo_step, 0)
                run(yb_lo, 3)
                run(stats1, 1)
                run(z0, 0)
                run(stats0, 0)
                run(z4, 3)
                run(stats4, 3)
                run(sj, 0)
                run(hstat, 2)
                run(x1T_lo, 0)
                run(H_step, 0)
                run(yf, 2)
                run(lk, 0)

            walk(dve, B, tick)

        @block.tensor
        def _(pe):
            def product(out, lhs, rhs, kt):
                for k in range(kt):
                    for m, (a, b) in enumerate(((0, 0), (0, 1), (1, 0))):
                        last = pe.matmul(out, lhs(k, a), rhs(k, b), start=(k == 0 and m == 0),
                                         stop=(k == kt - 1 and m == 2))
                return last

            def incidence_product(out, lhs, rhs, kt):
                for k in range(kt):
                    for b in range(2):
                        last = pe.matmul(out, lhs(k, b), rhs(k, b), start=(k == 0 and b == 0),
                                         stop=(k == kt - 1 and b == 1))
                return last

            def plain(out, lhs, rhs, kt):
                for k in range(kt):
                    last = pe.matmul(out, lhs(k), rhs(k), start=(k == 0), stop=(k == kt - 1))
                return last

            pe.wait_ge(ld_w0, 16 * 11)
            pe.wait_ge(p_rep, 1)
            pe.wait_ge(p_const, 3)
            for d in range(DT):
                plain(bank(0, 0)[:, d], lambda k: st_wq[:, k, tl(d)], lambda k: st_wk[:, k, :], DT)
                plain(bank(1, 0)[:, d, 0:P], lambda k: st_aVT[:, k, tl(d)], lambda k: rep_awi[:, k, :], DT)
                plain(bank(1, 1)[:, d, 0:P], lambda k: st_wq[:, k, tl(d)], lambda k: rep_bk[:, k, :], DT)
                plain(ps[3][:, 0, d:d + 1], lambda k: st_wk[:, k, tl(d)], lambda k: bq_col[:, k:k + 1], DT)
            plain(bank(2, 0)[:, 0], lambda k: rep_awj[:, k, :], lambda k: st_aVT[:, k, :], DT)
            plain(ps[3][:, 0, 2:3], lambda k: rep_bk[:, k, :], lambda k: bq_col[:, k:k + 1], DT)
            plain(ps[3][:, 0, 3:4], lambda k: rep_aws[:, k, :], lambda k: abv_col[:, k:k + 1], DT)
            pe.wait_ge(ld_w1, 16 * 11)
            plain(bank(2, 1)[:, 0], lambda k: rep_bet[:, k, :], lambda k: st_w2[:, k, :], HT_).then_inc(p_mm, 1)
            pe.wait_ge(p_rep, 2)
            plain(ps[3][:, 1, 0:D], lambda k: ones[:, :], lambda k: gam_w2[:, k, :], HT_).then_inc(p_mm, 1)
            pe.wait_ge(p_done, 1)

            def t(g, n, nn, l16):
                pe.wait_ge(s["xT_lo"], n)
                pe.wait_ge(s["banks_free"], n)
                qk = (qk_hi, qk_lo)
                for d in range(DT):
                    last = product(bank(g, 0)[:, d], lambda k, a: qk[a][:, k, tl(d)], lambda k, b: RA[g][:, b, k], DT)
                last.then_inc(s["t_ps"], 1)

            def sT(g, n, nn, l16):
                pe.wait_ge(s["t_lo"], n)
                for j in range(NT):
                    for k in range(DT):
                        pe.matmul(bank(g, 1)[:, j], row_rep[:, k, :], RA[g][:, 0, k], start=(k == 0), stop=False)
                    for k in range(DT):
                        for m, (a, b) in enumerate(((0, 0), (0, 1), (1, 0))):
                            last = pe.matmul(bank(g, 1)[:, j], RA[g][:, a, k, tl(j)], RB[g][:, b, k],
                                             start=False, stop=(k == DT - 1 and m == 2))
                last.then_inc(s["sT_ps"], 1)

            def v(g, n, nn, l16):
                pe.wait_ge(s["t_lo"], n)
                vw = (v_hi, v_lo)
                for j in range(NT):
                    last = product(bank(g, 0)[:, j], lambda k, a: RA[g][:, a, k, tl(j)], lambda k, b: vw[b][:, k, :], DT)
                last.then_inc(s["v_ps"], 1)

            def weighted(g):
                for i in range(NT):
                    last = product(ps[g][:, i, 0:DY], lambda k, a: RB[g][:, a, k, tl(i)], lambda k, b: Y[g][:, b, k, :], NT)
                return last

            def pv(g, n, nn, l16):
                pe.wait_ge(s["pT_lo"], n)
                pe.wait_ge(s["v_lo"], n)
                weighted(g).then_inc(s["pv_ps"], 1)

            def transpose(g):
                for d in range(DT):
                    for j in range(NT):
                        last = pe.transpose(bank(g, 0)[:, d, tl(j)], X[g][:, j, tl(d)], ident[:, :])
                return last

            def x1T(g, n, nn, l16):
                pe.wait_ge(s["x1"], n)
                transpose(g).then_inc(s["x1T_ps"], 1)

            def project(g, b, weight):
                for j in range(NT):
                    last = product(bank(g, b)[:, j], lambda k, a: RA[g][:, a, k, tl(j)], weight, DT)
                return last

            wk = (wk_hi, wk_lo)

            def y2(g, n, nn, l16):
                pe.wait_ge(s["x1T_lo"], n)
                project(g, 1, lambda k, c: wk[c][:, k, 2, :]).then_inc(s["y2_ps"], 1)

            def si(g, n, nn, l16):
                pe.wait_ge(s["x1T_lo"], n)
                sw = (si_hi, si_lo)
                product(bank(g, 0)[:, 0], lambda k, a: sw[a][:, k, :], lambda k, b: RA[g][:, b, k], DT)\
                    .then_inc(s["si_ps"], 1)

            def y1(g, n, nn, l16):
                pe.wait_ge(s["y2_lo"], n)
                project(g, 1, lambda k, c: wk[c][:, k, 1, :]).then_inc(s["y1_ps"], 1)

            def y0(g, n, nn, l16):
                pe.wait_ge(s["zs"], n)
                project(g, 0, lambda k, c: wk[c][:, k, 0, :]).then_inc(s["y0_ps"], 1)

            def z1(g, n, nn, l16):
                pe.wait_ge(s["T_lo"], n)
                pe.wait_ge(s["y1"], n)
                pe.wait_ge(s["y0"], n)
                weighted(g).then_inc(s["z1_ps"], 1)

            def z2(g, n, nn, l16):
                pe.wait_ge(s["w1_lo"], n)
                for i in range(NT):
                    last = product(bank(g, 0)[:, i], lambda k, a: RB[g][:, a, k, tl(i)], lambda k, b: RA[g][:, b, k], NT)
                last.then_inc(s["z2_ps"], 1)

            def m(g, n, nn, l16):
                pe.wait_ge(s["x2_lo"], n)
                pe.wait_ge(s["H"], n)
                for j in range(NT):
                    last = incidence_product(bank(g, 1)[:, j], lambda k, b: H[g][:, k, tl(j)],
                                             lambda k, b: RB[g][:, b, k], NT)
                last.then_inc(s["m_ps"], 1)

            def db(g, n, nn, l16):
                pe.wait_ge(s["diag"], n)
                pe.wait_ge(s["z1n"], n)
                for j in range(NT):
                    last = pe.matmul(ps[g][:, 0, tl(j)], ones[:, :], w_bc[g][:, tl(j)], start=True, stop=True)
                last.then_inc(s["db_ps"], 1)

            def uT(g, n, nn, l16):
                pe.wait_ge(s["m_lo"], n)
                pe.wait_ge(s["HT"], n)
                for d in range(DT):
                    last = incidence_product(bank(g, 1)[:, d], lambda k, b: RA[g][:, b, k, tl(d)],
                                             lambda k, b: HT[g][:, k, :], NT)
                last.then_inc(s["uT_ps"], 1)

            def h(g, n, nn, l16):
                pe.wait_ge(s["u_lo"], n)
                ww = (w1_hi, w1_lo)
                for c in range(HT_):
                    last = product(bank(g, c // 2)[:, c % 2], lambda k, a: ww[a][:, k, tl(c)],
                                   lambda k, b: RB[g][:, b, k], DT)
                last.then_inc(s["h_ps"], 1)

            def y(g, n, nn, l16):
                pe.wait_ge(s["r_lo"], n)
                parts, ww = (RA, RB), (w2_hi, w2_lo)
                for i in range(NT):
                    last = product(ps[g][:, i, 0:DY], lambda k, a: four(parts[a][g], k)[:, tl(i)],
                                   lambda k, b: ww[b][:, k, :], HT_)
                last.then_inc(s["y_ps"], 1)

            def ss(g, n, nn, l16):
                pe.wait_ge(s["sqs"], n)
                for i in range(NT):
                    last = pe.matmul(ps[g][:, i, D + 1:DY], F[g][:, 2, tl(i)], ones[:, 0:1], start=True, stop=True)
                last.then_inc(s["ss_ps"], 1)

            def m2(g, n, nn, l16):
                pe.wait_ge(s["yf_lo"], n)
                for j in range(NT):
                    last = incidence_product(bank(g, 0)[:, j], lambda k, b: H[g][:, k, tl(j)],
                                             lambda k, b: RA[g][:, b, k], NT)
                last.then_inc(s["m2_ps"], 1)

            def u2(g, n, nn, l16):
                pe.wait_ge(s["m2_lo"], n)
                for i in range(NT):
                    last = incidence_product(bank(g, 1)[:, i], lambda k, b: HT[g][:, k, tl(i)],
                                             lambda k, b: RB[g][:, b, k], NT)
                last.then_inc(s["u2_ps"], 1)

            def x3T(g, n, nn, l16):
                pe.wait_ge(s["x3"], n)
                transpose(g).then_inc(s["x3T_ps"], 1)

            w3 = (w3_hi, w3_lo)

            def yb(g, n, nn, l16):
                pe.wait_ge(s["x3T_lo"], n)
                project(g, 1, lambda k, c: w3[c][:, DT + k, :]).then_inc(s["yb_ps"], 1)

            def ya(g, n, nn, l16):
                pe.wait_ge(s["x3T_lo"], n)
                project(g, 0, lambda k, c: w3[c][:, k, :]).then_inc(s["ya_ps"], 1)

            def ag(g, n, nn, l16):
                pe.wait_ge(s["yb_lo"], n)
                pe.wait_ge(s["ya"], n)
                pe.wait_ge(s["aT_lo"], n)
                weighted(g).then_inc(s["ag_ps"], 1)

            def tick(run):
                run(y0, 1)
                run(m2, 3)
                run(uT, 2)
                run(y1, 1)
                run(u2, 3)
                run(z1, 1)
                run(t, 0)
                run(h, 2)
                run(sT, 0)
                run(x3T, 3)
                run(z2, 1)
                run(v, 0)
                run(yb, 3)
                run(ya, 3)
                run(pv, 0)
                run(db, 1)
                run(ag, 3)
                run(y, 2)
                run(ss, 2)
                run(x1T, 0)
                run(m, 1)
                run(si, 0)
                run(y2, 0)

            walk(pe, B, tick)


def kernel(**inputs):
    import numpy as np
    import concourse.bacc as bacc
    from concourse.bass_utils import run_bass_kernel_spmd

    a = {k: np.asarray(v) for k, v in inputs.items()}
    arrays = {
        "x": a["x"], "xT": a["x"].transpose(0, 2, 1), "adj": a["adj"], "adjT": a["adj"].transpose(0, 2, 1),
        "Wq": a["L0_gnn_Wq_w"], "bq": a["L0_gnn_Wq_b"], "Wkey": a["L0_gnn_Wk_w"], "bkey": a["L0_gnn_Wk_b"],
        "WvT": a["L0_gnn_Wv_w"].T, "bv": a["L0_gnn_Wv_b"],
        "aVT": a["L1_gnn_Wv"].T, "abv": a["L1_gnn_bv"], "aw": a["L1_gnn_aw"].reshape(-1), "ab": a["L1_gnn_ab"],
        "Wk": a["L1_gnn_Wk"], "bk": a["L1_gnn_bk"],
        "W1T": a["L2_gnn_W1"].T, "b1": a["L2_gnn_b1"], "gamma": a["L2_gnn_gamma"], "beta": a["L2_gnn_beta"],
        "W2T": a["L2_gnn_W2"].T, "b2": a["L2_gnn_b2"],
        "W3T": a["L3_gnn_W"].T,
    }
    nc = bacc.Bacc("TRN2", target_bir_lowering=False, num_devices=1)
    aps, feed = {}, {}
    for name, v in arrays.items():
        feed[f"in_{name}"] = np.ascontiguousarray(v)
        aps[name] = nc.dram_tensor(f"in_{name}", v.shape, F32, kind="ExternalInput").ap()
    aps["out"] = nc.dram_tensor("out_x", a["x"].shape, F32, kind="ExternalOutput").ap()
    build_graph_stack(nc, aps)
    r = run_bass_kernel_spmd(nc, [feed], core_ids=[0])
    return r.results[0]["out_x"]
```

```python
from contextlib import ExitStack

import concourse.bass as bass
from concourse import mybir

F32 = mybir.dt.float32
F32R = mybir.dt.float32r
ALU = mybir.AluOpType
ACT = mybir.ActivationFunctionType

P = 128
LN_EPS = 1e-5
TINY = 1.2e-38
G = 4
LAGS = 5

ADJ_AT = (32, 48, 64)


def walk(eng, B, tick):
    def peeled(k):
        def run(step, lag):
            m = k - lag
            if 0 <= m < B:
                step(m % G, m + 1, m + 1 + G, 16 * (m // G + 1),
                     [64 * (m // G) + at for at in ADJ_AT])
        tick(run, k)

    for k in range(G):
        peeled(k)
    with eng.Fori(G, B, G) as i:
        count = {o: eng.snap(i + (o + 1)) for o in range(1 - LAGS, 2 * G)}
        loads = {o: eng.snap(i * (16 // G) + (16 + 16 // G * o)) for o in (-G, 0)}
        adj_ats = {o: [eng.snap(i * (64 // G) + (at + 64 // G * o)) for at in ADJ_AT] for o in (-G, 0)}
        for q in range(G):
            def run(step, lag):
                o = q - lag
                step(o % G, count[o], count[o + G], loads[o - o % G], adj_ats[o - o % G])
            tick(run, None)
    for k in range(B, B + LAGS - 1):
        peeled(k)


def build_graph_stack(nc, A):
    B, N, D = A["x"].shape
    DH = A["W1T"].shape[1]
    K = A["Wk"].shape[0]
    NT = N // P
    DT = D // P
    HT_ = DH // P
    DY = D + 2
    assert NT == 2 and DT == 2 and HT_ == 4 and N == D == 256 and B % G == 0 and K == 3 and LAGS <= G + 1

    ctx = ExitStack()
    with ctx:
        def sb(name, shape, dt=F32):
            return ctx.enter_context(nc.sbuf_tensor(name, shape, dt))

        def sem(name):
            return ctx.enter_context(nc.semaphore(name))

        def per_slot(name, shape, dt=F32):
            return [sb(f"{name}{g}", shape, dt) for g in range(G)]

        qk_hi, qk_lo = sb("qk_hi", [P, DT, D], F32R), sb("qk_lo", [P, DT, D], F32R)
        v_hi, v_lo = sb("v_hi", [P, DT, D], F32R), sb("v_lo", [P, DT, D], F32R)
        wk_hi, wk_lo = sb("wk_hi", [P, DT, K, D], F32R), sb("wk_lo", [P, DT, K, D], F32R)
        w1_hi, w1_lo = sb("w1_hi", [P, DT, DH], F32R), sb("w1_lo", [P, DT, DH], F32R)
        w3_hi, w3_lo = sb("w3_hi", [P, 2 * DT, D], F32R), sb("w3_lo", [P, 2 * DT, D], F32R)
        si_hi, si_lo = sb("si_hi", [P, DT, P], F32R), sb("si_lo", [P, DT, P], F32R)
        w2_hi, w2_lo = sb("w2_hi", [P, HT_, DY], F32R), sb("w2_lo", [P, HT_, DY], F32R)
        row_rep = sb("row_rep", [P, DT, P], F32R)
        ident = sb("ident", [P, P])
        ones = sb("ones", [P, P])
        bv_bc = sb("bv_bc", [P, D])
        bk_bc = sb("bk_bc", [P, D])
        sj_bc = sb("sj_bc", [P, D])
        w2b_bc = sb("w2b_bc", [P, D])
        b2_bc = sb("b2_bc", [P, D])
        b1_col = sb("b1_col", [P, HT_])
        qk_col = sb("qk_col", [P, DT])
        bqbk = sb("bqbk", [P, 1])
        e_const = sb("e_const", [P, 1])
        cols = sb("cols", [P, 24])
        minus_half = sb("minus_half", [P, 2])
        eps_col = sb("eps_col", [P, 2])

        x = per_slot("x", [P, NT, D])
        xT = per_slot("xT", [P, DT, N])
        adj = per_slot("adj", [P, NT, N])
        adjT = per_slot("adjT", [P, NT, N])
        w_bc = per_slot("w_bc", [P, N])
        RA = per_slot("RA", [P, 2, 2, 256], F32R)
        RB = per_slot("RB", [P, 2, 2, 256], F32R)
        H = per_slot("H", [P, NT, N], F32R)
        HT = per_slot("HT", [P, NT, N], F32R)
        F = per_slot("F", [P, 4, 256])
        Y = per_slot("Y", [P, 2, NT, DY], F32R)
        R4 = per_slot("R4", [P, 4, 256])
        X = per_slot("X", [P, NT, D])
        sm = per_slot("sm", [P, 64])
        ps = [ctx.enter_context(nc.psum_tensor(f"ps{g}", [P, 2, 512], F32)) for g in range(G)]

        def stats(g, t):
            return sm[g][:, 6 * t:6 * t + 6]

        def mv(g):
            return sm[g][:, 12:16].rearrange("p (t c) -> p t c", c=2)

        def rstd(g):
            return sm[g][:, 16:18]

        def rinv(g):
            return sm[g][:, 18:20]

        def rsum(g):
            return sm[g][:, 20:22]

        def sj_col(g):
            return sm[g][:, 22:24]

        def deg(g):
            return sm[g][:, 24:28]

        def deg_mask(g):
            return sm[g][:, 28:32]

        def deg_safe(g):
            return sm[g][:, 32:36]

        def deg_inv(g):
            return sm[g][:, 36:40]

        def hmom(g):
            return sm[g][:, 40:44].rearrange("p (t c) -> p t c", c=2)

        def hmean2(g):
            return sm[g][:, 44:46]

        def hvar(g):
            return sm[g][:, 46:48]

        def veps(g):
            return sm[g][:, 48:50]

        def sjraw(g):
            return sm[g][:, 50:52]

        def neg_mean(g):
            return sm[g][:, 52:54]

        def nbias(g):
            return sm[g][:, 54:56]

        def bank(g, b):
            return ps[g][:, b, :].rearrange("p (t n) -> p t n", t=2)

        def tl(t):
            return slice(t * P, (t + 1) * P)

        def four(buf, part):
            return buf[:, part // 2, part % 2]

        ld_xT = [sem(f"ld_xT{g}") for g in range(G)]
        ld_x = [sem(f"ld_x{g}") for g in range(G)]
        ld_adj = [sem(f"ld_adj{g}") for g in range(G)]
        ld_adjT = [sem(f"ld_adjT{g}") for g in range(G)]
        stored = [sem(f"stored{g}") for g in range(G)]
        names = """xT_hi xT_lo xb t_ps t_hi t_lo sT_ps v_ps eT v_hi v_lo pT pT_hi pT_lo pv_ps inv0 z0
            st0 mv0  ve0 rs0 nb0 x1
            x1T_ps x1T_hi x1T_lo sjr sjc y2_ps y2_hi y2_lo si_ps zs lk e1 T T_hi T_lo y1_ps y0_ps y1 y0
            z1_ps den1 inv1 w1 w1_hi w1_lo z2_ps h1 z1n st1 mv1  ve1 rs1 nb1 x2
            H HT dn  dsafe drec dinv 
            x2_hi x2_lo x2b m_ps  m_hi m_lo  uT_ps u u_hi u_lo h_ps r sq r_hi r_lo sqa  sqs y_ps ss_ps
             hst hm2 hv ve2 rs2 yf yf_hi yf_lo m2_ps m2_hi m2_lo u2_ps z3 st3 mv3  ve3 rs3 nb3 x3
            x3T_ps x3T_hi x3T_lo yb_ps yb_hi yb_lo ya_ps ya aT_hi aT_lo ag_ps den4 inv4 agz
            banks_free st4 mv4  ve4 rs4 nb4 outp""".split()
        s = {name: sem(name) for name in names}
        stats_seen = sem("stats_seen")
        ld_qk, ld_score, ld_value, ld_layer1, ld_layer2, ld_layer3 = (
            sem("ld_qk"), sem("ld_score"), sem("ld_value"), sem("ld_layer1"), sem("ld_layer2"), sem("ld_layer3"))
        p_const = sem("p_const")
        p_rep = sem("p_rep")
        p_mm = sem("p_mm")
        p_ev = sem("p_ev")
        p_hi = sem("p_hi")
        p_done = sem("p_done")

        st_wq, st_wk = R4[2][:, 0:2, :], R4[2][:, 2:4, :]
        gam_w2 = R4[2]
        st_vT, st_aVT = R4[3][:, 0:2, :], R4[3][:, 2:4, :]
        st_kw = [X[2][:, :, :], R4[1][:, 0:2, :], R4[1][:, 2:4, :]]
        st_w1 = F[2][:, :, :].rearrange("p (k a) n -> p k (a n)", k=DT)
        st_w2 = F[3][:, :, :]
        st_w3 = R4[3]
        st_bk3 = R4[0][:, 0:3, :]
        rep_bk, rep_awj = X[0][:, :, 0:P], X[0][:, :, P:2 * P]
        rep_awi, rep_aws = X[1][:, :, 0:P], X[1][:, :, P:2 * P]
        rep_bet = X[3][:, :, :].rearrange("p t (a n) -> p (t a) n", a=2)
        mm_qk, mm_row = bank(3, 0), bank(3, 1)[:, 0].rearrange("p (t n) -> p t n", t=DT)
        mm_si, mm_sj = bank(2, 1)[:, 0].rearrange("p (t n) -> p t n", t=DT), bank(2, 1)[:, 1]
        mm_qk_col, mm_bqbk, mm_const = ps[1][:, 0, 0:2], ps[2][:, 0, 2:3], ps[2][:, 0, 3:4]
        mm_w2b, mm_w2_sum = bank(2, 0)[:, 1], bank(3, 1)[:, 1]
        bq_col, bk_col = cols[:, 0:2], cols[:, 2:4]
        awj_col, awi_col = cols[:, 4:6], cols[:, 6:8]
        abv_col = cols[:, 8:10]
        gam_col, bet_col = cols[:, 10:14], cols[:, 14:18]
        ab_col = cols[:, 18:19]
        aw_sum = cols[:, 20:22]

        block = ctx.enter_context(nc.Block())

        @block.sync
        def _(sp):
            def tiles(ap):
                return ap.rearrange("(t p) n -> p t n", p=P)

            def column(ap, k):
                return ap.rearrange("(t p) -> p t", p=P)[:, 0:k]

            def load(name, dst, sems, g):
                sp.dma_start(dst[g][:, :, :], tiles(A[name][g])).then_inc(sems[g], 16)

            def load_adj(g):
                load("adj", adj, ld_adj, g)
                sp.dma_start(w_bc[g][:, :], A["adj"][g, 0, :].partition_broadcast(P)).then_inc(ld_adj[g], 16)

            def weights(done, *pairs):
                with nc.allow_non_contiguous_dma(reason="weight vectors as columns, once"):
                    for dst, src in pairs:
                        sp.dma_start(dst, src).then_inc(done, 16)

            for g in range(G):
                sp.sem_inc(stored[g], 16)
            weights(ld_qk, (st_wq, tiles(A["Wq"])), (st_wk, tiles(A["Wkey"])))
            load("xT", xT, ld_xT, 0)
            weights(ld_score, (bq_col, column(A["bq"], DT)), (bk_col, column(A["bkey"], DT)))
            weights(ld_value, (st_vT, tiles(A["WvT"])), (bv_bc[:, :], A["bv"].partition_broadcast(P)))
            load("adjT", adjT, ld_adjT, 0)
            load("x", x, ld_x, 0)
            weights(ld_layer1, (st_aVT, tiles(A["aVT"])),
                    (awj_col, column(A["aw"][0:D], DT)), (awi_col, column(A["aw"][D:2 * D], DT)),
                    (abv_col, column(A["abv"], DT)), (ab_col, A["ab"].partition_broadcast(P)),
                    (st_kw[2], tiles(A["Wk"][2])), (st_kw[1], tiles(A["Wk"][1])), (st_kw[0], tiles(A["Wk"][0])),
                    (st_bk3, A["bk"].partition_broadcast(P)))
            load_adj(0)
            load("xT", xT, ld_xT, 1)
            weights(ld_layer2, (gam_col, column(A["gamma"], HT_)), (bet_col, column(A["beta"], HT_)),
                    (st_w2, tiles(A["W2T"])), (st_w1, tiles(A["W1T"])),
                    (b1_col[:, :], column(A["b1"], HT_)), (b2_bc[:, :], A["b2"].partition_broadcast(P)))
            for g in range(1, G):
                if g > 1:
                    load("xT", xT, ld_xT, g)
                load("adjT", adjT, ld_adjT, g)
                load("x", x, ld_x, g)
                load_adj(g)
            sp.wait_ge(p_done, 5)
            weights(ld_layer3, (st_w3[:, :, :], tiles(A["W3T"])))

            def slot(name, g):
                return A[name].rearrange("(j g) r n -> g j r n", g=G)[g]

            def graph(name, j, g):
                return slot(name, g)[bass.ds(j, 1), :, :].rearrange("a (t p) n -> p (a t) n", p=P)

            with sp.Fori(0, B // G - 1, 1) as j:
                for g in range(G):
                    n = sp.snap(j * G + (g + 1))
                    sp.wait_ge(s["xT_lo"], n)
                    sp.dma_start(xT[g][:, :, :], graph("xT", j + 1, g)).then_inc(ld_xT[g], 16)
                    sp.wait_ge(s["z0"], n)
                    sp.dma_start(x[g][:, :, :], graph("x", j + 1, g)).then_inc(ld_x[g], 16)
                    sp.wait_ge(s["u"], n)
                    sp.dma_start(adj[g][:, :, :], graph("adj", j + 1, g)).then_inc(ld_adj[g], 16)
                    sp.dma_start(w_bc[g][:, :],
                                 slot("adj", g)[bass.ds(j + 1, 1), 0, :].rearrange("a n -> (a n)").partition_broadcast(P))\
                        .then_inc(ld_adj[g], 16)
                    sp.wait_ge(s["aT_lo"], n)
                    sp.dma_start(adjT[g][:, :, :], graph("adjT", j + 1, g)).then_inc(ld_adjT[g], 16)
                    sp.wait_ge(s["outp"], n)
                    sp.dma_start(graph("out", j, g), R4[g][:, 2:4, :]).then_inc(stored[g], 16)
            for g in range(G):
                sp.wait_ge(s["outp"], B - G + g + 1)
                sp.dma_start(tiles(A["out"][B - G + g]), R4[g][:, 2:4, :]).then_inc(stored[g], 16)
            for g in range(G):
                sp.wait_ge(stored[g], 16 * (B // G + 1))

        @block.gpsimd
        def _(pool):
            pool.memset(ones[:, :], 1.0)
            pool.memset(eps_col[:, :], LN_EPS)
            pool.memset(minus_half[:, :], -0.5).then_inc(p_const, 1)
            pool.memset(ident[:, :], 0.0).then_inc(p_const, 1)
            pool.wait_ge(p_const, 2)
            pool.affine_select(out=ident[:, :], in_=ident[:, :], compare_op=ALU.not_equal, fill=1.0,
                               base=0, pattern=[[-1, P]], channel_multiplier=1).then_inc(p_const, 1)
            pool.wait_ge(p_const, 3)

            def low_part(lo, full, hi, done):
                pool.tensor_tensor(lo, full, hi.bitcast(F32), ALU.subtract).then_inc(s[done], 1)

            def rsqrt(l, n, g):
                pool.wait_ge(s["ve" + l], n)
                pool.tensor_tensor(rstd(g), veps(g), minus_half[:, :], ALU.pow).then_inc(s["rs" + l], 1)

            def norm_scalars(l, n, g):
                rsqrt(l, n, g)
                pool.wait_ge(s["rs" + l], n)
                pool.tensor_tensor(nbias(g), neg_mean(g), rstd(g), ALU.mult).then_inc(s["nb" + l], 1)

            def xT_lo(g, n, nn, l16, adj_at):
                pool.wait_ge(s["xT_hi"], n)
                low_part(RA[g][:, 1], xT[g][:, :, :], RA[g][:, 0], "xT_lo")

            def xb(g, n, nn, l16, adj_at):
                pool.wait_ge(ld_x[g], l16)
                pool.wait_ge(ld_value, 16 * 2)
                pool.tensor_tensor(x[g][:, :, :], x[g][:, :, :],
                                   bv_bc[:, None, :].to_broadcast([P, NT, D]), ALU.add).then_inc(s["xb"], 1)

            def pT(g, n, nn, l16, adj_at):
                pool.wait_ge(s["eT"], n)
                pool.wait_ge(ld_adjT[g], l16)
                pool.tensor_tensor(F[g][:, 0:2, :], F[g][:, 0:2, :], adjT[g][:, :, :], ALU.mult)\
                    .then_inc(s["pT"], 1)

            def pT_lo(g, n, nn, l16, adj_at):
                pool.wait_ge(s["pT_hi"], n)
                low_part(RB[g][:, 1], F[g][:, 0:2, :], RB[g][:, 0], "pT_lo")

            def rs0(g, n, nn, l16, adj_at):
                norm_scalars("0", n, g)

            def T(g, n, nn, l16, adj_at):
                pool.wait_ge(s["e1"], n)
                pool.tensor_tensor(F[g][:, 0:2, :], F[g][:, 0:2, :], adjT[g][:, :, :], ALU.mult)\
                    .then_inc(s["T"], 1)

            def T_lo(g, n, nn, l16, adj_at):
                pool.wait_ge(s["T_hi"], n)
                low_part(RB[g][:, 1], F[g][:, 0:2, :], RB[g][:, 0], "T_lo")

            def w1_lo(g, n, nn, l16, adj_at):
                pool.wait_ge(s["w1_hi"], n)
                low_part(RA[g][:, 1], R4[g][:, 0:2, :], RA[g][:, 0], "w1_lo")

            def rs1(g, n, nn, l16, adj_at):
                norm_scalars("1", n, g)

            def x2_lo(g, n, nn, l16, adj_at):
                pool.wait_ge(s["x2_hi"], n)
                low_part(RB[g][:, 1], X[g][:, :, :], RB[g][:, 0], "x2_lo")

            def u_lo(g, n, nn, l16, adj_at):
                pool.wait_ge(s["u_hi"], n)
                low_part(RB[g][:, 1], F[g][:, 0:2, :], RB[g][:, 0], "u_lo")

            def r_lo(g, n, nn, l16, adj_at):
                pool.wait_ge(s["r_hi"], n)
                low_part(RB[g][:, :, :, :].rearrange("p a b n -> p (a b) n"), R4[g][:, :, :],
                         RA[g][:, :, :, :].rearrange("p a b n -> p (a b) n"), "r_lo")

            def rs2(g, n, nn, l16, adj_at):
                pool.wait_ge(s["hv"], n)
                pool.tensor_tensor(veps(g), hvar(g), eps_col[:, :], ALU.add).then_inc(s["ve2"], 1)
                rsqrt("2", n, g)

            def yf_lo(g, n, nn, l16, adj_at):
                pool.wait_ge(s["yf_hi"], n)
                low_part(RA[g][:, 1], F[g][:, 2:4, :], RA[g][:, 0], "yf_lo")

            def rs3(g, n, nn, l16, adj_at):
                norm_scalars("3", n, g)

            def aT_lo(g, n, nn, l16, adj_at):
                pool.wait_ge(s["aT_hi"], n)
                low_part(RB[g][:, 1], adjT[g][:, :, :], RB[g][:, 0], "aT_lo")

            def rs4(g, n, nn, l16, adj_at):
                norm_scalars("4", n, g)

            def tick(run, k):
                if k == 2:
                    pool.wait_ge(p_done, 7)
                run(xT_lo, 0)
                run(rs1, 2)
                run(rs2, 3)
                run(x2_lo, 2)
                run(yf_lo, 3)
                run(T, 1)
                run(rs4, 4)
                run(T_lo, 1)
                run(aT_lo, 3)
                run(rs3, 3)
                run(u_lo, 2)
                run(pT, 0)
                run(w1_lo, 1)
                run(pT_lo, 0)
                run(xb, 0)
                run(r_lo, 2)
                run(rs0, 0)

            walk(pool, B, tick)

        @block.scalar
        def _(act):
            def high_part(hi, full, done):
                act.activation(hi, full, ACT.Copy).then_inc(s[done], 1)

            def normalise(dst, src, l, done, n, g):
                act.wait_ge(s["nb" + l], n)
                for t in range(NT):
                    last = act.activation(dst[:, t, :], src[:, t, :], ACT.Identity,
                                          bias=nbias(g)[:, t:t + 1], scale=rstd(g)[:, t:t + 1])
                last.then_inc(s[done], 1)

            def layer1_high():
                act.wait_ge(ld_layer1, 16 * 9)
                for k in range(K):
                    last = act.activation(wk_hi[:, :, k, :], st_kw[k], ACT.Copy)
                last.then_inc(p_hi, 1)

            def layer2_high():
                act.wait_ge(ld_layer2, 16 * 6)
                act.activation(w1_hi[:, :, :], st_w1, ACT.Copy).then_inc(p_hi, 1)

            def layer3_high():
                act.wait_ge(ld_layer3, 16)
                act.activation(w3_hi[:, :, :], st_w3[:, :, :], ACT.Copy).then_inc(p_hi, 1)

            def xT_hi(g, n, nn, l16, adj_at):
                act.wait_ge(ld_xT[g], l16)
                high_part(RA[g][:, 0], xT[g][:, :, :], "xT_hi")

            def t_hi(g, n, nn, l16, adj_at):
                act.wait_ge(s["t_ps"], n)
                for d in range(DT):
                    last = act.activation(RB[g][:, 0, d], bank(g, 0)[:, d], ACT.Identity, bias=qk_col[:, d:d + 1])
                last.then_inc(s["t_hi"], 1)

            def eT(g, n, nn, l16, adj_at):
                act.wait_ge(s["sT_ps"], n)
                act.activation(F[g][:, 0:2, :], bank(g, 1), ACT.Exp, bias=bqbk[:, 0:1]).then_inc(s["eT"], 1)

            def v_hi_step(g, n, nn, l16, adj_at):
                act.wait_ge(s["v_ps"], n)
                high_part(Y[g][:, 0, :, 0:D], bank(g, 0), "v_hi")

            def pT_hi(g, n, nn, l16, adj_at):
                act.wait_ge(s["pT"], n)
                high_part(RB[g][:, 0], F[g][:, 0:2, :], "pT_hi")

            def x1(g, n, nn, l16, adj_at):
                normalise(X[g], F[g][:, 2:4, :], "0", "x1", n, g)

            def x1T_hi(g, n, nn, l16, adj_at):
                act.wait_ge(s["x1T_ps"], n)
                high_part(RA[g][:, 0], bank(g, 0), "x1T_hi")

            def y2_hi(g, n, nn, l16, adj_at):
                act.wait_ge(s["y2_ps"], n)
                high_part(Y[g][:, 0, :, 0:D], bank(g, 1), "y2_hi")

            def zs(g, n, nn, l16, adj_at):
                act.wait_ge(s["si_ps"], n)
                act.wait_ge(s["sjc"], n)
                for t in range(NT):
                    last = act.activation(F[g][:, t, :], bank(g, 0)[:, 0], ACT.Identity, bias=sj_col(g)[:, t:t + 1])
                last.then_inc(s["zs"], 1)

            def e1(g, n, nn, l16, adj_at):
                act.wait_ge(s["lk"], n)
                act.activation(F[g][:, 0:2, :], F[g][:, 2:4, :], ACT.Exp).then_inc(s["e1"], 1)

            def T_hi(g, n, nn, l16, adj_at):
                act.wait_ge(s["T"], n)
                high_part(RB[g][:, 0], F[g][:, 0:2, :], "T_hi")

            def y1_sb(g, n, nn, l16, adj_at):
                act.wait_ge(s["y1_ps"], n)
                act.activation(R4[g][:, 0:2, :], bank(g, 1), ACT.Copy).then_inc(s["y1"], 1)

            def w1_hi_step(g, n, nn, l16, adj_at):
                act.wait_ge(s["w1"], n)
                high_part(RA[g][:, 0], R4[g][:, 0:2, :], "w1_hi")

            def x2(g, n, nn, l16, adj_at):
                normalise(X[g], F[g][:, 0:2, :], "1", "x2", n, g)

            def x2_hi(g, n, nn, l16, adj_at):
                act.wait_ge(s["x2"], n)
                high_part(RB[g][:, 0], X[g][:, :, :], "x2_hi")

            def m_hi(g, n, nn, l16, adj_at):
                act.wait_ge(s["m_ps"], n)
                for t in range(NT):
                    last = act.activation(RA[g][:, 0, t], bank(g, 1)[:, t], ACT.Copy, scale=deg_inv(g)[:, 2 + t:3 + t])
                last.then_inc(s["m_hi"], 1)

            def d_out(g, n, nn, l16, adj_at):
                act.wait_ge(s["dinv"], n)
                with nc.allow_non_contiguous_dma(reason="256 numbers, one or two per partition"):
                    act.dma_start(A["inv_degree"][g].rearrange("(t p) -> p t", p=P), deg_inv(g)[:, 0:NT])\
                        .then_inc(ld_adj[g], 16)

            def d_in(g, n, nn, l16, adj_at):
                act.wait_ge(ld_adj[g], adj_at[1])
                act.dma_start(w_bc[g][:, :], A["inv_degree"][g].partition_broadcast(P)).then_inc(ld_adj[g], 16)

            def u_hi(g, n, nn, l16, adj_at):
                act.wait_ge(s["u"], n)
                high_part(RB[g][:, 0], F[g][:, 0:2, :], "u_hi")

            def r(g, n, nn, l16, adj_at):
                act.wait_ge(s["h_ps"], n)
                for k in range(HT_):
                    last = act.activation(R4[g][:, k, :], bank(g, k // 2)[:, k % 2], ACT.Relu, bias=b1_col[:, k:k + 1])
                last.then_inc(s["r"], 1)

            def sq(g, n, nn, l16, adj_at):
                act.wait_ge(s["r"], n)
                act.wait_ge(s["u_lo"], n)
                act.activation(F[g][:, :, :], R4[g][:, :, :], ACT.Square).then_inc(s["sq"], 1)

            def r_hi(g, n, nn, l16, adj_at):
                act.wait_ge(s["r"], n)
                high_part(RA[g][:, :, :, :].rearrange("p a b n -> p (a b) n"), R4[g][:, :, :], "r_hi")

            def yf_hi(g, n, nn, l16, adj_at):
                act.wait_ge(s["yf"], n)
                high_part(RA[g][:, 0], F[g][:, 2:4, :], "yf_hi")

            def m2_hi(g, n, nn, l16, adj_at):
                act.wait_ge(s["m2_ps"], n)
                for t in range(NT):
                    last = act.activation(RB[g][:, 0, t], bank(g, 0)[:, t], ACT.Copy, scale=deg_inv(g)[:, 2 + t:3 + t])
                last.then_inc(s["m2_hi"], 1)

            def x3(g, n, nn, l16, adj_at):
                normalise(X[g], F[g][:, 0:2, :], "3", "x3", n, g)

            def x3T_hi(g, n, nn, l16, adj_at):
                act.wait_ge(s["x3T_ps"], n)
                high_part(RA[g][:, 0], bank(g, 0), "x3T_hi")

            def yb_hi(g, n, nn, l16, adj_at):
                act.wait_ge(s["yb_ps"], n)
                high_part(Y[g][:, 0, :, 0:D], bank(g, 1), "yb_hi")

            def ya_sb(g, n, nn, l16, adj_at):
                act.wait_ge(s["ya_ps"], n)
                act.activation(R4[g][:, 0:2, :], bank(g, 0), ACT.Copy).then_inc(s["ya"], 1)

            def aT_hi(g, n, nn, l16, adj_at):
                act.wait_ge(s["u2_ps"], n)
                high_part(RB[g][:, 0], adjT[g][:, :, :], "aT_hi")

            def outp(g, n, nn, l16, adj_at):
                normalise(R4[g][:, 2:4, :], F[g][:, 2:4, :], "4", "outp", n, g)

            def tick(run, k):
                if k == 2:
                    act.wait_ge(p_done, 7)
                run(xT_hi, 0)
                run(x1, 1)
                run(x1T_hi, 1)
                run(x2, 2)
                run(x2_hi, 2)
                run(zs, 1)
                run(yf_hi, 3)
                run(y2_hi, 1)
                run(e1, 1)
                run(m_hi, 2)
                run(m2_hi, 3)
                if k == 0:
                    act.wait_ge(p_done, 2)
                run(t_hi, 0)
                if k == 0:
                    layer1_high()
                run(T_hi, 1)
                run(y1_sb, 1)
                if k == 1:
                    layer3_high()
                run(aT_hi, 3)
                run(outp, 4)
                run(eT, 0)
                run(u_hi, 2)
                run(x3, 3)
                run(v_hi_step, 0)
                run(w1_hi_step, 1)
                run(pT_hi, 0)
                if k == 0:
                    layer2_high()
                run(x3T_hi, 3)
                run(d_out, 1)
                run(r, 2)
                run(r_hi, 2)
                run(sq, 2)
                run(yb_hi, 3)
                run(ya_sb, 3)
                run(d_in, 1)

            walk(act, B, tick)

        @block.vector
        def _(dve):
            ev = [0]

            def step(ins):
                ins.then_inc(p_ev, 1)
                ev[0] += 1
                dve.wait_ge(p_ev, ev[0])

            def repeat(rep, col, kt):
                for k in range(kt):
                    last = dve.tensor_scalar(rep[:, k, :], ones[:, :], col[:, k:k + 1], None, ALU.mult)
                return last

            def split(hi, lo, full):
                step(dve.tensor_copy(hi, full))
                return dve.tensor_tensor(lo, full, hi.bitcast(F32), ALU.subtract)

            dve.sem_inc(s["banks_free"], G)
            dve.wait_ge(ld_score, 16 * 2)
            dve.wait_ge(p_const, 1)
            repeat(rep_bk, bk_col, DT).then_inc(p_rep, 1)
            dve.wait_ge(p_mm, 1)
            split(qk_hi[:, :, :], qk_lo[:, :, :], mm_qk).then_inc(p_done, 1)
            dve.wait_ge(p_mm, 2)
            dve.tensor_copy(qk_col[:, :], mm_qk_col).then_inc(p_done, 1)
            for lo_zero in [Y[g][:, 1, :, D:DY] for g in range(G)] + [w2_lo[:, :, D:DY]]:
                dve.memset(lo_zero.bitcast(F32), 0.0)
            for hi_one in [Y[g][:, 0, :, D:D + 1] for g in range(G)] + [w2_hi[:, :, D:D + 1]]:
                dve.memset(hi_one.bitcast(F32), 1.0)
            for hi_zero in [Y[g][:, 0, :, D + 1:DY] for g in range(G)] + [w2_hi[:, :, D + 1:DY]]:
                dve.memset(hi_zero.bitcast(F32), 0.0)
            dve.wait_ge(ld_value, 16 * 2)
            split(v_hi[:, :, :], v_lo[:, :, :], st_vT).then_inc(p_done, 1)
            dve.wait_ge(p_done, 3)

            def score_weights():
                dve.wait_ge(p_mm, 3)
                dve.tensor_copy(row_rep[:, :, :], mm_row)
                dve.tensor_copy(bqbk[:, :], mm_bqbk).then_inc(p_done, 1)

            def layer1_operands():
                dve.wait_ge(ld_layer1, 16 * 9)
                repeat(rep_awj, awj_col, DT)
                repeat(rep_awi, awi_col, DT)
                step(dve.tensor_tensor(aw_sum, awj_col, awi_col, ALU.add))
                repeat(rep_aws, aw_sum, DT).then_inc(p_rep, 1)

            def layer1_biases():
                step(dve.tensor_tensor(bk_bc[:, :], st_bk3[:, 0, :], st_bk3[:, 1, :], ALU.add))
                step(dve.tensor_tensor(bk_bc[:, :], bk_bc[:, :], st_bk3[:, 2, :], ALU.add))

            def layer1_folded():
                dve.wait_ge(p_mm, 4)
                dve.tensor_copy(sj_bc[:, :], mm_sj)
                dve.tensor_tensor(e_const[:, :], mm_const, ab_col, ALU.add)
                step(dve.tensor_copy(si_hi[:, :, :], mm_si))
                dve.tensor_tensor(si_lo[:, :, :], mm_si, si_hi[:, :, :].bitcast(F32), ALU.subtract)\
                    .then_inc(p_done, 1)
                dve.wait_ge(p_done, 5)

            def layer1_weights():
                dve.wait_ge(p_hi, 1)
                for k in range(K):
                    dve.tensor_tensor(wk_lo[:, :, k, :], st_kw[k], wk_hi[:, :, k, :].bitcast(F32), ALU.subtract)

            def layer2_operands():
                dve.wait_ge(ld_layer2, 16 * 6)
                repeat(rep_bet, bet_col, HT_)
                for k in range(HT_):
                    last = dve.tensor_scalar(gam_w2[:, k, :], st_w2[:, k, :], gam_col[:, k:k + 1], None, ALU.mult)
                last.then_inc(p_rep, 1)

            def layer2_weights():
                dve.wait_ge(p_hi, 2)
                dve.tensor_tensor(w1_lo[:, :, :], st_w1, w1_hi[:, :, :].bitcast(F32), ALU.subtract).then_inc(p_done, 1)

            def layer2_folded():
                dve.wait_ge(p_mm, 5)
                dve.tensor_copy(w2b_bc[:, :], mm_w2b)
                for k in range(HT_):
                    last = dve.scalar_tensor_tensor(st_w2[:, k, :], mm_w2_sum, -1.0 / DH, gam_w2[:, k, :],
                                                    ALU.mult, ALU.add)
                step(last)

            def layer2_split():
                split(w2_hi[:, :, 0:D], w2_lo[:, :, 0:D], st_w2)

            def layer3_weights():
                dve.wait_ge(p_hi, 3)
                dve.tensor_tensor(w3_lo[:, :, :], st_w3[:, :, :], w3_hi[:, :, :].bitcast(F32), ALU.subtract)\
                    .then_inc(p_done, 1)

            def layer_norm_stats(src, l, n, g):
                for t in range(NT):
                    last = dve.bn_stats(stats(g, t), src[:, t, :])
                last.then_inc(s["st" + l], 1)
                dve.wait_ge(s["st" + l], n)
                dve.sem_inc(stats_seen, 1)
                for t in range(NT):
                    last = dve.bn_aggr(mv(g)[:, t, :], stats(g, t))
                last.then_inc(s["mv" + l], 1)
                dve.wait_ge(s["mv" + l], n)
                dve.tensor_scalar(neg_mean(g), mv(g)[:, :, 0], -1.0, None, ALU.mult)
                dve.tensor_scalar(veps(g), mv(g)[:, :, 1], LN_EPS, None, ALU.add).then_inc(s["ve" + l], 1)

            def low_part(lo, full, hi, done):
                dve.tensor_tensor(lo, full, hi.bitcast(F32), ALU.subtract).then_inc(s[done], 1)

            def t_lo(g, n, nn, l16, adj_at):
                dve.wait_ge(s["t_hi"], n)
                for d in range(DT):
                    last = dve.scalar_tensor_tensor(RB[g][:, 1, d], bank(g, 0)[:, d], qk_col[:, d:d + 1],
                                                    RB[g][:, 0, d].bitcast(F32), ALU.add, ALU.subtract)
                last.then_inc(s["t_lo"], 1)

            def v_lo_step(g, n, nn, l16, adj_at):
                dve.wait_ge(s["v_hi"], n)
                low_part(Y[g][:, 1, :, 0:D], bank(g, 0), Y[g][:, 0, :, 0:D], "v_lo")

            def H_step(g, n, nn, l16, adj_at):
                dve.wait_ge(ld_adj[g], adj_at[0])
                dve.tensor_scalar(H[g][:, :, :], adj[g][:, :, :], 0.0, None, ALU.not_equal).then_inc(s["H"], 1)

            def HT_step(g, n, nn, l16, adj_at):
                dve.wait_ge(ld_adjT[g], l16)
                for t in range(NT):
                    last = dve.tensor_scalar(HT[g][:, t, :], adjT[g][:, t, :], 0.0, None, ALU.not_equal,
                                             ALU.add, accum_out=deg(g)[:, 2 + t:3 + t])
                last.then_inc(s["HT"], 1)

            def dn(g, n, nn, l16, adj_at):
                dve.wait_ge(s["H"], n)
                for t in range(NT):
                    last = dve.scalar_tensor_tensor(adj[g][:, t, :], H[g][:, t, :].bitcast(F32), 1.0,
                                                    w_bc[g][:, :], ALU.mult, ALU.mult,
                                                    accum_out=deg(g)[:, t:t + 1])
                last.then_inc(s["dn"], 1)

            def dinv(g, n, nn, l16, adj_at):
                dve.wait_ge(s["HT"], n)
                dve.wait_ge(s["dn"], n)
                dve.tensor_scalar(deg_mask(g), deg(g), 0.0, None, ALU.is_gt)
                dve.tensor_scalar(deg_safe(g), deg(g), TINY, None, ALU.max).then_inc(s["dsafe"], 1)
                dve.wait_ge(s["dsafe"], n)
                dve.reciprocal(deg_safe(g), deg_safe(g)).then_inc(s["drec"], 1)
                dve.wait_ge(s["drec"], n)
                dve.tensor_tensor(deg_inv(g), deg_safe(g), deg_mask(g), ALU.mult).then_inc(s["dinv"], 1)

            def z0(g, n, nn, l16, adj_at):
                dve.wait_ge(s["pv_ps"], n)
                dve.reciprocal(rinv(g), ps[g][:, :, D]).then_inc(s["inv0"], 1)
                dve.wait_ge(s["inv0"], n)
                dve.wait_ge(s["xb"], n)
                for t in range(NT):
                    last = dve.scalar_tensor_tensor(F[g][:, 2 + t, :], ps[g][:, t, 0:D], rinv(g)[:, t:t + 1],
                                                    x[g][:, t, :], ALU.mult, ALU.add)
                last.then_inc(s["z0"], 1)

            def stats0(g, n, nn, l16, adj_at):
                dve.wait_ge(s["z0"], n)
                layer_norm_stats(F[g][:, 2:4, :], "0", n, g)

            def sj(g, n, nn, l16, adj_at):
                dve.wait_ge(s["x1"], n)
                for t in range(NT):
                    last = dve.scalar_tensor_tensor(F[g][:, 2 + t, :], X[g][:, t, :], 1.0, sj_bc[:, :],
                                                    ALU.mult, ALU.mult, accum_out=sjraw(g)[:, t:t + 1])
                last.then_inc(s["sjr"], 1)
                dve.wait_ge(s["sjr"], n)
                dve.tensor_scalar(sj_col(g), sjraw(g), e_const[:, 0:1], None, ALU.add).then_inc(s["sjc"], 1)

            def x1T_lo(g, n, nn, l16, adj_at):
                dve.wait_ge(s["x1T_hi"], n)
                low_part(RA[g][:, 1], bank(g, 0), RA[g][:, 0], "x1T_lo")

            def y2_lo(g, n, nn, l16, adj_at):
                dve.wait_ge(s["y2_hi"], n)
                low_part(Y[g][:, 1, :, 0:D], bank(g, 1), Y[g][:, 0, :, 0:D], "y2_lo")

            def lk(g, n, nn, l16, adj_at):
                dve.wait_ge(s["zs"], n)
                dve.scalar_tensor_tensor(F[g][:, 2:4, :], F[g][:, 0:2, :], 0.2, F[g][:, 0:2, :],
                                         ALU.mult, ALU.max).then_inc(s["lk"], 1)

            def y0_sb(g, n, nn, l16, adj_at):
                dve.wait_ge(s["y0_ps"], n)
                dve.wait_ge(stored[g], l16)
                dve.tensor_tensor(R4[g][:, 2:4, :], bank(g, 0),
                                  bk_bc[:, None, :].to_broadcast([P, NT, D]), ALU.add).then_inc(s["y0"], 1)

            def w1(g, n, nn, l16, adj_at):
                dve.wait_ge(s["z1_ps"], n)
                dve.tensor_scalar(rsum(g), ps[g][:, :, D], 1e-12, None, ALU.add).then_inc(s["den1"], 1)
                dve.wait_ge(s["den1"], n)
                dve.reciprocal(rinv(g), rsum(g)).then_inc(s["inv1"], 1)
                dve.wait_ge(s["inv1"], n)
                for t in range(NT):
                    last = dve.scalar_tensor_tensor(R4[g][:, t, :], ps[g][:, t, 0:D], rinv(g)[:, t:t + 1],
                                                    R4[g][:, t, :], ALU.mult, ALU.add)
                last.then_inc(s["w1"], 1)

            def h1(g, n, nn, l16, adj_at):
                dve.wait_ge(s["z2_ps"], n)
                for t in range(NT):
                    last = dve.scalar_tensor_tensor(F[g][:, 2 + t, :], bank(g, 0)[:, t], rinv(g)[:, t:t + 1],
                                                    R4[g][:, 2 + t, :], ALU.mult, ALU.add)
                last.then_inc(s["h1"], 1)
                dve.wait_ge(s["h1"], n)
                dve.scalar_tensor_tensor(F[g][:, 0:2, :], F[g][:, 2:4, :], 0.0, X[g][:, :, :],
                                         ALU.max, ALU.add).then_inc(s["z1n"], 1)

            def stats1(g, n, nn, l16, adj_at):
                dve.wait_ge(s["z1n"], n)
                layer_norm_stats(F[g][:, 0:2, :], "1", n, g)

            def m_lo(g, n, nn, l16, adj_at):
                dve.wait_ge(s["m_hi"], n)
                for t in range(NT):
                    last = dve.scalar_tensor_tensor(RA[g][:, 1, t], bank(g, 1)[:, t], deg_inv(g)[:, 2 + t:3 + t],
                                                    RA[g][:, 0, t].bitcast(F32), ALU.mult, ALU.subtract)
                last.then_inc(s["m_lo"], 1)

            def x2b(g, n, nn, l16, adj_at):
                dve.wait_ge(s["x2_lo"], n)
                dve.scalar_tensor_tensor(X[g][:, :, :], X[g][:, :, :], 2.0,
                                         b2_bc[:, None, :].to_broadcast([P, NT, D]), ALU.mult, ALU.add)\
                    .then_inc(s["x2b"], 1)

            def u(g, n, nn, l16, adj_at):
                dve.wait_ge(s["uT_ps"], n)
                dve.wait_ge(ld_adj[g], adj_at[2])
                dve.tensor_tensor(F[g][:, 0:2, :], bank(g, 1), w_bc[g][:, None, :].to_broadcast([P, 2, D]),
                                  ALU.mult).then_inc(s["u"], 1)

            def sqs(g, n, nn, l16, adj_at):
                dve.wait_ge(s["sq"], n)
                dve.tensor_tensor(F[g][:, 0:2, :], F[g][:, 0:2, :], F[g][:, 2:4, :], ALU.add).then_inc(s["sqa"], 1)
                dve.wait_ge(s["sqa"], n)
                dve.tensor_tensor(F[g][:, 2, :], F[g][:, 0, :], F[g][:, 1, :], ALU.add).then_inc(s["sqs"], 1)

            def hstat(g, n, nn, l16, adj_at):
                dve.wait_ge(s["ss_ps"], n)
                dve.tensor_scalar(hmom(g), ps[g][:, :, D:DY], 1.0 / DH, None, ALU.mult).then_inc(s["hst"], 1)
                dve.wait_ge(s["hst"], n)
                dve.tensor_tensor(hmean2(g), hmom(g)[:, :, 0], hmom(g)[:, :, 0], ALU.mult).then_inc(s["hm2"], 1)
                dve.wait_ge(s["hm2"], n)
                dve.tensor_tensor(hvar(g), hmom(g)[:, :, 1], hmean2(g), ALU.subtract).then_inc(s["hv"], 1)

            def yf(g, n, nn, l16, adj_at):
                dve.wait_ge(s["rs2"], n)
                for t in range(NT):
                    last = dve.scalar_tensor_tensor(F[g][:, 2 + t, :], ps[g][:, t, 0:D], rstd(g)[:, t:t + 1],
                                                    w2b_bc[:, :], ALU.mult, ALU.add)
                last.then_inc(s["yf"], 1)

            def m2_lo(g, n, nn, l16, adj_at):
                dve.wait_ge(s["m2_hi"], n)
                for t in range(NT):
                    last = dve.scalar_tensor_tensor(RB[g][:, 1, t], bank(g, 0)[:, t], deg_inv(g)[:, 2 + t:3 + t],
                                                    RB[g][:, 0, t].bitcast(F32), ALU.mult, ALU.subtract)
                last.then_inc(s["m2_lo"], 1)

            def z3(g, n, nn, l16, adj_at):
                dve.wait_ge(s["u2_ps"], n)
                dve.wait_ge(s["x2b"], n)
                for t in range(NT):
                    last = dve.scalar_tensor_tensor(F[g][:, t, :], bank(g, 1)[:, t], deg_inv(g)[:, t:t + 1],
                                                    X[g][:, t, :], ALU.mult, ALU.add)
                last.then_inc(s["z3"], 1)

            def stats3(g, n, nn, l16, adj_at):
                dve.wait_ge(s["z3"], n)
                layer_norm_stats(F[g][:, 0:2, :], "3", n, g)

            def x3T_lo(g, n, nn, l16, adj_at):
                dve.wait_ge(s["x3T_hi"], n)
                low_part(RA[g][:, 1], bank(g, 0), RA[g][:, 0], "x3T_lo")

            def yb_lo(g, n, nn, l16, adj_at):
                dve.wait_ge(s["yb_hi"], n)
                low_part(Y[g][:, 1, :, 0:D], bank(g, 1), Y[g][:, 0, :, 0:D], "yb_lo")

            def z4(g, n, nn, l16, adj_at):
                dve.wait_ge(s["ag_ps"], n)
                dve.tensor_scalar(rsum(g), ps[g][:, :, D], 1e-6, None, ALU.max).then_inc(s["den4"], 1)
                dve.wait_ge(s["den4"], n)
                dve.reciprocal(rinv(g), rsum(g)).then_inc(s["inv4"], 1)
                dve.wait_ge(s["inv4"], n)
                for t in range(NT):
                    last = dve.scalar_tensor_tensor(F[g][:, t, :], ps[g][:, t, 0:D], rinv(g)[:, t:t + 1],
                                                    R4[g][:, t, :], ALU.mult, ALU.add)
                last.then_inc(s["agz"], 1)
                dve.wait_ge(s["agz"], n)
                dve.scalar_tensor_tensor(F[g][:, 2:4, :], F[g][:, 0:2, :], 0.0, X[g][:, :, :],
                                         ALU.max, ALU.add).then_inc(s["banks_free"], 1)

            def stats4(g, n, nn, l16, adj_at):
                dve.wait_ge(s["banks_free"], nn)
                layer_norm_stats(F[g][:, 2:4, :], "4", n, g)

            def tick(run, k):
                if k == 2:
                    dve.wait_ge(p_done, 7)
                run(sqs, 3)
                run(yb_lo, 4)
                run(hstat, 3)
                run(x1T_lo, 1)
                run(sj, 1)
                run(yf, 3)
                run(z4, 4)
                run(lk, 1)
                run(y2_lo, 1)
                run(y0_sb, 1)
                if k == 1:
                    layer2_split()
                    layer2_weights()
                run(stats4, 4)
                run(m2_lo, 3)
                run(m_lo, 2)
                run(t_lo, 0)
                if k == 0:
                    score_weights()
                    layer1_operands()
                    layer1_biases()
                    layer1_weights()
                run(z3, 3)
                run(stats3, 3)
                run(u, 2)
                run(x2b, 2)
                run(w1, 1)
                if k == 1:
                    layer3_weights()
                run(H_step, 1)
                run(HT_step, 0)
                run(dn, 1)
                run(dinv, 1)
                run(x3T_lo, 3)
                run(v_lo_step, 0)
                if k == 0:
                    layer1_folded()
                    layer2_operands()
                run(h1, 1)
                run(z0, 0)
                run(stats0, 0)
                if k == 0:
                    layer2_folded()
                run(stats1, 1)

            walk(dve, B, tick)

        @block.tensor
        def _(pe):
            def product(out, lhs, rhs, kt):
                for k in range(kt):
                    for m, (a, b) in enumerate(((0, 0), (0, 1), (1, 0))):
                        last = pe.matmul(out, lhs(k, a), rhs(k, b), start=(k == 0 and m == 0),
                                         stop=(k == kt - 1 and m == 2))
                return last

            def incidence_product(out, lhs, rhs, kt):
                for k in range(kt):
                    for b in range(2):
                        last = pe.matmul(out, lhs(k, b), rhs(k, b), start=(k == 0 and b == 0),
                                         stop=(k == kt - 1 and b == 1))
                return last

            def plain(out, lhs, rhs, kt):
                for k in range(kt):
                    last = pe.matmul(out, lhs(k), rhs(k), start=(k == 0), stop=(k == kt - 1))
                return last

            pe.wait_ge(ld_qk, 16 * 2)
            for d in range(DT):
                last = plain(mm_qk[:, d], lambda k: st_wq[:, k, tl(d)], lambda k: st_wk[:, k, :], DT)
            last.then_inc(p_mm, 1)
            pe.wait_ge(ld_score, 16 * 2)
            for d in range(DT):
                last = plain(mm_qk_col[:, d:d + 1], lambda k: st_wk[:, k, tl(d)], lambda k: bq_col[:, k:k + 1], DT)
            last.then_inc(p_mm, 1)

            def fold_scores():
                pe.wait_ge(p_rep, 1)
                for d in range(DT):
                    plain(mm_row[:, d], lambda k: st_wq[:, k, tl(d)], lambda k: rep_bk[:, k, :], DT)
                plain(mm_bqbk, lambda k: rep_bk[:, k, :], lambda k: bq_col[:, k:k + 1], DT).then_inc(p_mm, 1)

            def fold_layer1():
                pe.wait_ge(p_rep, 2)
                pe.wait_ge(ld_layer1, 16 * 9)
                for d in range(DT):
                    plain(mm_si[:, d], lambda k: st_aVT[:, k, tl(d)], lambda k: rep_awi[:, k, :], DT)
                plain(mm_sj, lambda k: rep_awj[:, k, :], lambda k: st_aVT[:, k, :], DT)
                plain(mm_const, lambda k: rep_aws[:, k, :], lambda k: abv_col[:, k:k + 1], DT).then_inc(p_mm, 1)

            def fold_layer2():
                pe.wait_ge(p_rep, 3)
                pe.wait_ge(ld_layer2, 16 * 6)
                plain(mm_w2b, lambda k: rep_bet[:, k, :], lambda k: st_w2[:, k, :], HT_)
                plain(mm_w2_sum, lambda k: ones[:, :], lambda k: gam_w2[:, k, :], HT_).then_inc(p_mm, 1)

            pe.wait_ge(p_const, 3)

            def t(g, n, nn, l16, adj_at):
                pe.wait_ge(s["xT_lo"], n)
                pe.wait_ge(s["banks_free"], n)
                qk = (qk_hi, qk_lo)
                for d in range(DT):
                    last = product(bank(g, 0)[:, d], lambda k, a: qk[a][:, k, tl(d)], lambda k, b: RA[g][:, b, k], DT)
                last.then_inc(s["t_ps"], 1)

            def sT(g, n, nn, l16, adj_at):
                pe.wait_ge(s["t_lo"], n)
                for j in range(NT):
                    for k in range(DT):
                        pe.matmul(bank(g, 1)[:, j], row_rep[:, k, :], RA[g][:, 0, k], start=(k == 0), stop=False)
                    for k in range(DT):
                        for m, (a, b) in enumerate(((0, 0), (0, 1), (1, 0))):
                            last = pe.matmul(bank(g, 1)[:, j], RA[g][:, a, k, tl(j)], RB[g][:, b, k],
                                             start=False, stop=(k == DT - 1 and m == 2))
                last.then_inc(s["sT_ps"], 1)

            def v(g, n, nn, l16, adj_at):
                pe.wait_ge(s["t_lo"], n)
                vw = (v_hi, v_lo)
                for j in range(NT):
                    last = product(bank(g, 0)[:, j], lambda k, a: RA[g][:, a, k, tl(j)], lambda k, b: vw[b][:, k, :], DT)
                last.then_inc(s["v_ps"], 1)

            def weighted(g):
                for i in range(NT):
                    last = product(ps[g][:, i, 0:DY], lambda k, a: RB[g][:, a, k, tl(i)], lambda k, b: Y[g][:, b, k, :], NT)
                return last

            def pv(g, n, nn, l16, adj_at):
                pe.wait_ge(s["pT_lo"], n)
                pe.wait_ge(s["v_lo"], n)
                weighted(g).then_inc(s["pv_ps"], 1)

            def transpose(g):
                for d in range(DT):
                    for j in range(NT):
                        last = pe.transpose(bank(g, 0)[:, d, tl(j)], X[g][:, j, tl(d)], ident[:, :])
                return last

            def x1T(g, n, nn, l16, adj_at):
                pe.wait_ge(s["x1"], n)
                transpose(g).then_inc(s["x1T_ps"], 1)

            def project(g, b, weight):
                for j in range(NT):
                    last = product(bank(g, b)[:, j], lambda k, a: RA[g][:, a, k, tl(j)], weight, DT)
                return last

            wk = (wk_hi, wk_lo)

            def y2(g, n, nn, l16, adj_at):
                pe.wait_ge(s["x1T_lo"], n)
                project(g, 1, lambda k, c: wk[c][:, k, 2, :]).then_inc(s["y2_ps"], 1)

            def si(g, n, nn, l16, adj_at):
                pe.wait_ge(s["x1T_lo"], n)
                sw = (si_hi, si_lo)
                product(bank(g, 0)[:, 0], lambda k, a: sw[a][:, k, :], lambda k, b: RA[g][:, b, k], DT)\
                    .then_inc(s["si_ps"], 1)

            def y1(g, n, nn, l16, adj_at):
                pe.wait_ge(s["y2_lo"], n)
                project(g, 1, lambda k, c: wk[c][:, k, 1, :]).then_inc(s["y1_ps"], 1)

            def y0(g, n, nn, l16, adj_at):
                pe.wait_ge(s["zs"], n)
                project(g, 0, lambda k, c: wk[c][:, k, 0, :]).then_inc(s["y0_ps"], 1)

            def z1(g, n, nn, l16, adj_at):
                pe.wait_ge(s["T_lo"], n)
                pe.wait_ge(s["y1"], n)
                pe.wait_ge(s["y0"], n)
                weighted(g).then_inc(s["z1_ps"], 1)

            def z2(g, n, nn, l16, adj_at):
                pe.wait_ge(s["w1_lo"], n)
                for i in range(NT):
                    last = product(bank(g, 0)[:, i], lambda k, a: RB[g][:, a, k, tl(i)], lambda k, b: RA[g][:, b, k], NT)
                last.then_inc(s["z2_ps"], 1)

            def m(g, n, nn, l16, adj_at):
                pe.wait_ge(s["x2_lo"], n)
                pe.wait_ge(s["H"], n)
                for j in range(NT):
                    last = incidence_product(bank(g, 1)[:, j], lambda k, b: H[g][:, k, tl(j)],
                                             lambda k, b: RB[g][:, b, k], NT)
                last.then_inc(s["m_ps"], 1)

            def uT(g, n, nn, l16, adj_at):
                pe.wait_ge(s["m_lo"], n)
                pe.wait_ge(s["HT"], n)
                for d in range(DT):
                    last = incidence_product(bank(g, 1)[:, d], lambda k, b: RA[g][:, b, k, tl(d)],
                                             lambda k, b: HT[g][:, k, :], NT)
                last.then_inc(s["uT_ps"], 1)

            def h(g, n, nn, l16, adj_at):
                pe.wait_ge(s["u_lo"], n)
                ww = (w1_hi, w1_lo)
                for c in range(HT_):
                    last = product(bank(g, c // 2)[:, c % 2], lambda k, a: ww[a][:, k, tl(c)],
                                   lambda k, b: RB[g][:, b, k], DT)
                last.then_inc(s["h_ps"], 1)

            def y(g, n, nn, l16, adj_at):
                pe.wait_ge(s["r_lo"], n)
                parts, ww = (RA, RB), (w2_hi, w2_lo)
                for i in range(NT):
                    last = product(ps[g][:, i, 0:DY], lambda k, a: four(parts[a][g], k)[:, tl(i)],
                                   lambda k, b: ww[b][:, k, :], HT_)
                last.then_inc(s["y_ps"], 1)

            def ss(g, n, nn, l16, adj_at):
                pe.wait_ge(s["sqs"], n)
                for i in range(NT):
                    last = pe.matmul(ps[g][:, i, D + 1:DY], F[g][:, 2, tl(i)], ones[:, 0:1], start=True, stop=True)
                last.then_inc(s["ss_ps"], 1)

            def m2(g, n, nn, l16, adj_at):
                pe.wait_ge(s["yf_lo"], n)
                for j in range(NT):
                    last = incidence_product(bank(g, 0)[:, j], lambda k, b: H[g][:, k, tl(j)],
                                             lambda k, b: RA[g][:, b, k], NT)
                last.then_inc(s["m2_ps"], 1)

            def u2(g, n, nn, l16, adj_at):
                pe.wait_ge(s["m2_lo"], n)
                for i in range(NT):
                    last = incidence_product(bank(g, 1)[:, i], lambda k, b: HT[g][:, k, tl(i)],
                                             lambda k, b: RB[g][:, b, k], NT)
                last.then_inc(s["u2_ps"], 1)

            def x3T(g, n, nn, l16, adj_at):
                pe.wait_ge(s["x3"], n)
                transpose(g).then_inc(s["x3T_ps"], 1)

            w3 = (w3_hi, w3_lo)

            def yb(g, n, nn, l16, adj_at):
                pe.wait_ge(s["x3T_lo"], n)
                project(g, 1, lambda k, c: w3[c][:, DT + k, :]).then_inc(s["yb_ps"], 1)

            def ya(g, n, nn, l16, adj_at):
                pe.wait_ge(s["x3T_lo"], n)
                project(g, 0, lambda k, c: w3[c][:, k, :]).then_inc(s["ya_ps"], 1)

            def ag(g, n, nn, l16, adj_at):
                pe.wait_ge(s["yb_lo"], n)
                pe.wait_ge(s["ya"], n)
                pe.wait_ge(s["aT_lo"], n)
                weighted(g).then_inc(s["ag_ps"], 1)

            def tick(run, k):
                if k == 2:
                    pe.wait_ge(p_done, 7)
                run(x1T, 1)
                run(ss, 3)
                run(ag, 4)
                if k == 1:
                    pe.wait_ge(p_done, 5)
                run(si, 1)
                if k == 1:
                    pe.wait_ge(p_done, 5)
                run(y2, 1)
                run(y0, 1)
                run(m, 2)
                run(m2, 3)
                if k == 0:
                    pe.wait_ge(p_done, 1)
                run(t, 0)
                if k == 0:
                    fold_scores()
                run(y1, 1)
                run(u2, 3)
                run(uT, 2)
                if k == 0:
                    pe.wait_ge(p_done, 4)
                run(sT, 0)
                run(z1, 1)
                if k == 0:
                    pe.wait_ge(p_done, 3)
                run(v, 0)
                if k == 0:
                    fold_layer1()
                run(x3T, 3)
                if k == 2:
                    pe.wait_ge(p_done, 6)
                run(h, 2)
                run(z2, 1)
                run(pv, 0)
                if k == 0:
                    fold_layer2()
                run(yb, 3)
                run(ya, 3)
                run(y, 2)

            walk(pe, B, tick)


def kernel(**inputs):
    import numpy as np
    import concourse.bacc as bacc
    from concourse.bass_utils import run_bass_kernel_spmd

    a = {k: np.asarray(v) for k, v in inputs.items()}
    arrays = {
        "x": a["x"], "xT": a["x"].transpose(0, 2, 1), "adj": a["adj"], "adjT": a["adj"].transpose(0, 2, 1),
        "Wq": a["L0_gnn_Wq_w"], "bq": a["L0_gnn_Wq_b"], "Wkey": a["L0_gnn_Wk_w"], "bkey": a["L0_gnn_Wk_b"],
        "WvT": a["L0_gnn_Wv_w"].T, "bv": a["L0_gnn_Wv_b"],
        "aVT": a["L1_gnn_Wv"].T, "abv": a["L1_gnn_bv"], "aw": a["L1_gnn_aw"].reshape(-1), "ab": a["L1_gnn_ab"],
        "Wk": a["L1_gnn_Wk"], "bk": a["L1_gnn_bk"],
        "W1T": a["L2_gnn_W1"].T, "b1": a["L2_gnn_b1"], "gamma": a["L2_gnn_gamma"], "beta": a["L2_gnn_beta"],
        "W2T": a["L2_gnn_W2"].T, "b2": a["L2_gnn_b2"],
        "W3T": a["L3_gnn_W"].T,
    }
    nc = bacc.Bacc("TRN2", target_bir_lowering=False, num_devices=1)
    aps, feed = {}, {}
    for name, v in arrays.items():
        feed[f"in_{name}"] = np.ascontiguousarray(v)
        aps[name] = nc.dram_tensor(f"in_{name}", v.shape, F32, kind="ExternalInput").ap()
    aps["out"] = nc.dram_tensor("out_x", a["x"].shape, F32, kind="ExternalOutput").ap()
    aps["inv_degree"] = nc.dram_tensor("inv_degree", (G, a["x"].shape[1]), F32, kind="Internal").ap()
    build_graph_stack(nc, aps)
    r = run_bass_kernel_spmd(nc, [feed], core_ids=[0])
    return r.results[0]["out_x"]
```
